# Optimizing a Trainium2 kernel written in Bass

```python
import numpy as np
import jax
import jax.numpy as jnp

def _softmax(x, axis=-1):
    return jax.nn.softmax(x, axis=axis)
def _gelu(x):
    return jax.nn.gelu(x, approximate=True)
def _silu(x):
    return jax.nn.silu(x)
def _sigmoid(x):
    return jax.nn.sigmoid(x)
def _layernorm(x, axis=-1, eps=1e-5):
    m = jnp.mean(x, axis=axis, keepdims=True)
    v = jnp.var(x, axis=axis, keepdims=True)
    return (x - m) / jnp.sqrt(v + eps)
def _scatter_add(tgt, idx, src, axis=0):
    return tgt.at[idx].add(src)
def _segment_sum(src, seg, n):
    return jax.ops.segment_sum(src, seg, n)

kernel_name = 'mk_adj_preln_d2_adj_512_b2dbd4'

def setup_inputs(seed: int = 0):
    np.random.seed(seed)
    _w = jnp.asarray
    def _rec_inputs():
        import jax
        import jax.numpy as jnp
        _gk = jax.random.key(seed)
        x = -0.0002928 + 1 * jax.random.normal(jax.random.fold_in(_gk, 1), (64, 256, 512), jnp.float32)
        _w = (1.0 + jnp.arange(256, dtype=jnp.float32)) ** -0.5
        _w = _w / _w.mean()
        _pij = jnp.clip(0.03125 * _w[:, None] * _w[None, :], 0.0, 1.0)
        _a = jax.random.uniform(jax.random.fold_in(_gk, 2), (256, 256)) < _pij
        _af = _a.astype(jnp.float32)
        adj = _af
        return x, adj
    x, adj = _rec_inputs()
    def _L0_gnn_setup():
        import jax, jax.numpy as jnp
        import numpy as np
        B, N, D, H = (4, 2048, 512, 8)
        HD = D // H
        key = jax.random.key(seed)
        ks = jax.random.split(key, 10)
        x = jax.random.normal(ks[0], (B, N, D), dtype=jnp.float32)
        adj = (jax.random.uniform(ks[1], (N, N)) < 0.1).astype(jnp.float32)
        s = 1.0 / np.sqrt(D)
        Wq = jax.random.normal(ks[2], (D, D), dtype=jnp.float32) * s
        Wk = jax.random.normal(ks[3], (D, D), dtype=jnp.float32) * s
        Wv = jax.random.normal(ks[4], (D, D), dtype=jnp.float32) * s
        Wo = jax.random.normal(ks[5], (D, D), dtype=jnp.float32) * s
        bq = jnp.zeros((D,), jnp.float32)
        bk = jnp.zeros((D,), jnp.float32)
        bv = jnp.zeros((D,), jnp.float32)
        bo = jnp.zeros((D,), jnp.float32)
        return {'x': x, 'adj': adj, 'Wq': Wq, 'bq': bq, 'Wk': Wk, 'bk': bk, 'Wv': Wv, 'bv': bv, 'Wo': Wo, 'bo': bo}
    _L0_gnn_all = _L0_gnn_setup()
    _L0_gnn_in = {k: v for k, v in _L0_gnn_all.items() if k in ('Wq', 'bq', 'Wk', 'bk', 'Wv', 'bv', 'Wo', 'bo', )}
    del _L0_gnn_all

    def _L1_gnn_setup():
        import jax, jax.numpy as jnp
        import numpy as np
        B, N, D, O = (8, 4096, 512, 512)
        key = jax.random.key(seed)
        k1, k2, k3, k4 = jax.random.split(key, 4)
        x = jax.random.normal(k1, (B, N, D), dtype=jnp.float32)
        adj = jax.random.uniform(k2, (N, N), dtype=jnp.float32)
        weight = jax.random.normal(k3, (D, O), dtype=jnp.float32) * 0.02
        bias = jax.random.normal(k4, (O,), dtype=jnp.float32) * 0.02
        return {'x': x, 'adj': adj, 'weight': weight, 'bias': bias}
    _L1_gnn_all = _L1_gnn_setup()
    _L1_gnn_in = {k: v for k, v in _L1_gnn_all.items() if k in ('weight', 'bias', )}
    del _L1_gnn_all

    return {
        "x": x,
        "adj": adj,
        "L0_gnn_Wq": _L0_gnn_in["Wq"],
        "L0_gnn_bq": _L0_gnn_in["bq"],
        "L0_gnn_Wk": _L0_gnn_in["Wk"],
        "L0_gnn_bk": _L0_gnn_in["bk"],
        "L0_gnn_Wv": _L0_gnn_in["Wv"],
        "L0_gnn_bv": _L0_gnn_in["bv"],
        "L0_gnn_Wo": _L0_gnn_in["Wo"],
        "L0_gnn_bo": _L0_gnn_in["bo"],
        "L1_gnn_weight": _L1_gnn_in["weight"],
        "L1_gnn_bias": _L1_gnn_in["bias"],
    }

def reference(x, adj, L0_gnn_Wq, L0_gnn_bq, L0_gnn_Wk, L0_gnn_bk, L0_gnn_Wv, L0_gnn_bv, L0_gnn_Wo, L0_gnn_bo, L1_gnn_weight, L1_gnn_bias):
    import jax
    import jax.numpy as jnp
    def _L0_gnn_ref(x, adj, Wq, bq, Wk, bk, Wv, bv, Wo, bo):
        import jax, jax.numpy as jnp
        import numpy as np
        B, N, D, H = (4, 2048, 512, 8)
        HD = D // H
        b, n, d = x.shape
        q = (x @ Wq + bq).reshape(b, n, H, HD)
        k = (x @ Wk + bk).reshape(b, n, H, HD)
        v = (x @ Wv + bv).reshape(b, n, H, HD)
        scores = jnp.einsum('bqhd,bkhd->bhqk', q, k) / jnp.sqrt(jnp.float32(HD))
        scores = scores + (1.0 - adj)[None, None, :, :] * -1000000000.0
        attn = jax.nn.softmax(scores, axis=-1)
        out = jnp.einsum('bhqk,bkhd->bqhd', attn, v).reshape(b, n, d)
        return out @ Wo + bo

    def _L1_gnn_ref(x, adj, weight, bias):
        import jax, jax.numpy as jnp
        import numpy as np
        B, N, D, O = (8, 4096, 512, 512)
        y = jnp.einsum('nm,bmd->bnd', adj, x)
        out = jnp.einsum('bnd,do->bno', y, weight) + bias
        return out

    h = jnp.maximum(_layernorm(x, axis=-1), 0.0)
    x = x + _L0_gnn_ref(h, adj, L0_gnn_Wq, L0_gnn_bq, L0_gnn_Wk, L0_gnn_bk, L0_gnn_Wv, L0_gnn_bv, L0_gnn_Wo, L0_gnn_bo)
    h = jnp.maximum(_layernorm(x, axis=-1), 0.0)
    x = x + _L1_gnn_ref(h, adj, L1_gnn_weight, L1_gnn_bias)
    return x


_drawn_inputs = setup_inputs


def setup_inputs(seed=0):
    import zlib

    import numpy as np

    out = dict(_drawn_inputs(seed))
    spreads = {'L0_gnn_bq': (0.0, 0.8),
     'L0_gnn_bk': (0.0, 0.8),
     'L0_gnn_bv': (0.0, 0.1),
     'L0_gnn_bo': (0.0, 0.1)}
    factors = {'L1_gnn_bias': 7.348}
    for name, (base, spread) in spreads.items():
        noise = np.random.default_rng([zlib.crc32(name.encode()), seed]).standard_normal(out[name].shape)
        drawn = base * np.exp(spread * noise) if base else spread * noise
        out[name] = jnp.asarray(drawn.astype(out[name].dtype))
    for name, factor in factors.items():
        out[name] = (out[name] * factor).astype(out[name].dtype)
    return out
```

```python
from contextlib import ExitStack

import concourse.bass as bass
from concourse import mybir

F32 = mybir.dt.float32
F32R = mybir.dt.float32r
ALU = mybir.AluOpType
ACT = mybir.ActivationFunctionType

P = 128
EPS = 1e-5
MASK = 1e9
HUGE = 3.0e38


def adjacency_layers(nc, x, adj, Wq, bq, Wk, bk, Wv, bv, Wo, bo, W1, b1, out):
    NB, N, D = x.shape
    H = 8
    HD = D // H
    NT = N // P
    DC = D // P
    PAIRS = H // 2
    RING = 4
    SCALE = 1.0 / HD ** 0.5
    assert HD * 2 == P and PAIRS == DC and N * 2 == D and SCALE == 0.125

    FIRST, END = 2, NB - 2
    assert (END - FIRST) % RING == 0

    FILLS = [
        (0, "qk", 0), (0, "v", 0), (0, "v", 1),
        (1, "qk", 0), (1, "wo", 0), (1, "wo", 1),
        (2, "qk", 0), (2, "ht", 0), (2, "ht", 1), (2, "w1", 0), (2, "w1", 1),
        (3, "qk", 0), (3, "y", 0), (3, "y", 1),
    ]
    LAG = {"v": 0, "wo": 1, "ht": -1, "w1": 2, "y": 1}
    BANKS = 3
    STAGES = 2

    def exists(batch):
        return not isinstance(batch, int) or 0 <= batch < NB

    def pair_exists(g):
        return not isinstance(g, int) or 0 <= g < NB * PAIRS

    def fill_count(i, f):
        slot, kind, part = FILLS[f]
        if kind == "qk":
            g = i * PAIRS + (slot + 1)
            return g + 1 if pair_exists(g) else None
        n = i - LAG[kind]
        return n * 2 + (part + 1) if exists(n) else None

    def fills_of(i, slot):
        return [f for f, fill in enumerate(FILLS) if fill[0] == slot and fill_count(i, f) is not None]

    def bank_user_before(i, f):
        bank, k, t = f % BANKS, f, i
        while True:
            k -= 1
            if k < 0:
                k, t = len(FILLS) - 1, t - 1
                if isinstance(t, int) and t < -1:
                    return None
            if k % BANKS == bank and fill_count(t, k) is not None:
                return FILLS[k][1], fill_count(t, k)

    def times(eng, step):
        for i in range(-1, FIRST):
            step(i, i % RING)
        with eng.Fori(0, (END - FIRST) // RING) as m:
            for j in range(RING):
                step(m * RING + (FIRST + j), (FIRST + j) % RING)
        for i in range(END, NB + 2):
            step(i, i % RING)

    with ExitStack() as ctx:
        def sb(name, shape, dt=F32):
            return ctx.enter_context(nc.sbuf_tensor(name, shape, dt))

        def sem(name):
            return ctx.enter_context(nc.semaphore(name))

        def split_pair(name, shape):
            return sb(name + "_hi", shape, F32R), sb(name + "_lo", shape, F32R)

        wq, wk, wv, wo, w1 = (split_pair(n, [P, DC, D]) for n in ("wq", "wk", "wv", "wo", "w1"))
        adjT = split_pair("adjT", [P, NT, N])
        mask = sb("mask", [P, NT, N])
        cbias = sb("cbias", [P, D])
        obias = sb("obias", [P, D])
        ident = sb("ident", [P, P])
        stage = sb("stage", [P, STAGES, DC, D])
        bias_rows = sb("bias_rows", [3 * DC, P])
        bias_cols = sb("bias_cols", [P, 3 * DC])
        bqs = sb("bqs", [P, DC])
        ones = sb("ones", [1, P])
        nhalf, eps = sb("nhalf", [P, NT]), sb("eps", [P, NT])

        xr = sb("xr", [P, RING, NT, D])
        h = sb("h", [P, NT, D])
        hT = split_pair("hT", [P, DC, N])
        qT = split_pair("qT", [P, 2, N])
        kT = split_pair("kT", [P, 2, N])
        v = split_pair("v", [P, 2, NT, D])
        logit = sb("logit", [P, 2, NT, N])
        adjn = logit[:, 0, :, :]
        bvb = logit[:, 1, :, :].rearrange("p a (b c) -> p (a b) c", c=P)
        low = sb("low", [P, 2 * NT])
        prob = sb("prob", [P, 2, NT, N])
        rows = prob[0:1, :, :, :].rearrange("p a b c -> p a (b c)")
        total = sb("total", [P, 2 * NT])
        rtotal = sb("rtotal", [P, 2 * NT])
        pT = split_pair("pT", [P, 2, NT, N])
        oT = split_pair("oT", [P, DC, N])
        z = sb("z", [P, NT, D])
        h2 = split_pair("h2", [P, NT, D])
        yT = split_pair("yT", [P, DC, N])
        st1 = sb("st1", [P, NT, 6]); mv1 = sb("mv1", [P, NT, 2]); rs1 = sb("rs1", [P, NT]); ve1 = sb("ve1", [P, NT])
        st2 = sb("st2", [P, NT, 6]); mv2 = sb("mv2", [P, NT, 2]); rs2 = sb("rs2", [P, NT]); ve2 = sb("ve2", [P, NT])

        def bank(name):
            return ctx.enter_context(nc.psum_tensor(name, [P, 512], F32))
        dense = [bank(f"dense{b}") for b in range(BANKS)]
        score = [bank(f"score{e}") for e in range(2)]
        probT = [bank(f"probT{e}") for e in range(2)]
        attn = bank("attn")

        x_loaded = [sem(f"x_loaded{r}") for r in range(RING)]
        x_stored = [sem(f"x_stored{r}") for r in range(RING)]
        w_loaded = [sem(f"w_loaded{n}") for n in range(5)]
        adj_loaded, bias_loaded = sem("adj_loaded"), sem("bias_loaded")
        ident_ready, ones_ready, powers_ready = sem("ident_ready"), sem("ones_ready"), sem("powers_ready")
        w_hi, w_lo = sem("w_hi"), sem("w_lo")
        adj_turned, adj_hi, adj_lo = sem("adj_turned"), sem("adj_hi"), sem("adj_lo")
        mask_ready, bias_ready = sem("mask_ready"), sem("bias_ready")
        bias_turned, bias_cols_ready = sem("bias_turned"), sem("bias_cols_ready")
        bias_filled, cbias_ready = sem("bias_filled"), sem("cbias_ready")
        KINDS = ("qk", "v", "wo", "ht", "w1", "y")
        filled = {k: sem(f"{k}_filled") for k in KINDS}
        hi_done = {k: sem(f"{k}_hi_done") for k in ("qk", "v", "ht", "y")}
        drained = {k: sem(f"{k}_drained") for k in KINDS}
        score_filled, logit_ready, exp_done = sem("score_filled"), sem("logit_ready"), sem("exp_done")
        rtotal_ready, prob_ready = sem("rtotal_ready"), sem("prob_ready")
        probT_filled, pT_hi_done, pT_ready = sem("probT_filled"), sem("pT_hi_done"), sem("pT_ready")
        attn_filled, oT_hi_done, oT_ready = sem("attn_filled"), sem("oT_hi_done"), sem("oT_ready")
        stats1, mv1_ready, rs1_ready, h_ready, xc_ready = (sem(n) for n in ("stats1", "mv1_ready", "rs1_ready", "h_ready", "xc_ready"))
        stats2, mv2_ready, rs2_ready, z_ready, xb_ready = (sem(n) for n in ("stats2", "mv2_ready", "rs2_ready", "z_ready", "xb_ready"))
        var1_ready, var2_ready = sem("var1_ready"), sem("var2_ready")
        h2_hi_done, h2_ready = sem("h2_hi_done"), sem("h2_ready")

        def f32(ap):
            return ap.bitcast(F32)

        WEIGHTS = [(wq, Wq, -SCALE), (wk, Wk, 1.0), (wv, Wv, 1.0), (wo, Wo, 1.0), (w1, W1, 1.0)]

        block = ctx.enter_context(nc.Block())

        @block.sync
        def _(sp):
            def load_x(b, r):
                sp.dma_start(xr[:, r, :, :], x[b].rearrange("(t p) d -> p t d", p=P)).then_inc(x_loaded[r], 16)

            def load_w(n):
                sp.dma_start(stage[:, n % STAGES, :, :], WEIGHTS[n][1].rearrange("(c p) n -> p c n", p=P)).then_inc(w_loaded[n], 16)

            load_x(0, 0)
            load_w(0)
            load_w(1)
            sp.dma_start(adjn[:, :, :], adj.rearrange("(t p) m -> p t m", p=P)).then_inc(adj_loaded, 16)
            load_x(1, 1)
            for n in range(STAGES, len(WEIGHTS)):
                sp.wait_ge(w_lo, n - 1)
                if n == 3 + 1:
                    load_x(2, 2)
                    load_x(3, 3)
                load_w(n)

            def step(i, r):
                if exists(i - 2):
                    sp.wait_ge(drained["w1"], (i - 2) * NT + NT)
                    s = (r - 2) % RING
                    sp.dma_start(out[i - 2].rearrange("(t p) d -> p t d", p=P), xr[:, s, :, :]).then_inc(x_stored[s], 16)
                    if exists(i + 2):
                        sp.wait_ge(x_stored[s], (i - 2) * 4 + (16 - 4 * s))
                        load_x(i + 2, s)

            times(sp, step)
            for s in range(RING):
                sp.wait_ge(x_stored[s], 16 * (NB // RING))

        @block.gpsimd
        def _(pool):
            for n, b in enumerate((bq, bk, bv)):
                pool.dma_start(bias_rows[n * DC:(n + 1) * DC, :], b.rearrange("(c p) -> c p", p=P)).then_inc(bias_loaded, 16)
            pool.dma_start(rows[:, 0, :], bo.rearrange("(a n) -> a n", a=1)).then_inc(bias_loaded, 16)
            pool.dma_start(rows[:, 1, :], b1.rearrange("(a n) -> a n", a=1)).then_inc(bias_loaded, 16)
            pool.memset(nhalf[:, :], -0.5).then_inc(powers_ready, 1)
            pool.memset(eps[:, :], EPS).then_inc(powers_ready, 1)
            pool.memset(ident[:, :], 0.0).then_inc(ident_ready, 1)
            pool.memset(ones[:, :], 1.0).then_inc(ones_ready, 1)
            pool.wait_ge(ident_ready, 1)
            pool.affine_select(out=ident[:, :], in_=ident[:, :], compare_op=ALU.not_equal, fill=1.0,
                               base=0, pattern=[[-1, P]], channel_multiplier=1).then_inc(ident_ready, 1)
            pool.wait_ge(powers_ready, 2)

            def norm_scale(mv, mv_ready, ve, var_ready, rs, rs_ready, n):
                pool.wait_ge(mv_ready, (n + 1) * NT)
                pool.tensor_tensor(ve[:, :], mv[:, :, 1], eps[:, :], ALU.add).then_inc(var_ready, 1)
                pool.wait_ge(var_ready, n + 1)
                pool.tensor_tensor(rs[:, :], ve[:, :], nhalf[:, :], ALU.pow).then_inc(rs_ready, 1)

            def step(i, r):
                for c in range(PAIRS):
                    g = i * PAIRS + c
                    if pair_exists(g):
                        for e in range(2):
                            if e == 0:
                                pool.wait_ge(rtotal_ready, g + 1)
                            pool.tensor_tensor(
                                prob[:, e, :, :], prob[:, e, :, :],
                                rtotal[:, e * NT:(e + 1) * NT].unsqueeze(2).to_broadcast((P, NT, N)),
                                ALU.mult).then_inc(prob_ready, 1)
                    if c == 0 and exists(i + 1):
                        norm_scale(mv1, mv1_ready, ve1, var1_ready, rs1, rs1_ready, i + 1)
                    if c == 1 and exists(i + 1):
                        pool.wait_ge(h_ready, (i + 2) * NT)
                        if isinstance(i, int) and i == -1:
                            pool.wait_ge(cbias_ready, 1)
                        s = (r + 1) % RING
                        for t in range(NT):
                            pool.tensor_tensor(xr[:, s, t, :], xr[:, s, t, :], cbias[:, :], ALU.add).then_inc(xc_ready, 1)
                    if c == 1 and exists(i - 1):
                        norm_scale(mv2, mv2_ready, ve2, var2_ready, rs2, rs2_ready, i - 1)
                    if c == 2 and exists(i - 1):
                        pool.wait_ge(z_ready, i * NT)
                        s = (r - 1) % RING
                        for t in range(NT):
                            pool.tensor_tensor(xr[:, s, t, :], xr[:, s, t, :], obias[:, :], ALU.add).then_inc(xb_ready, 1)

            times(pool, step)

        @block.scalar
        def _(act):
            for n, (w, _, scale) in enumerate(WEIGHTS):
                act.wait_ge(w_loaded[n], 16)
                act.activation(w[0][:, :, :], stage[:, n % STAGES, :, :], ACT.Copy, scale=scale).then_inc(w_hi, 1)
                if n == 0:
                    act.wait_ge(adj_turned, 1)
                    act.activation(adjT[0][:, :, :].rearrange("p a b -> p (a b)"), score[0][:, :], ACT.Copy).then_inc(adj_hi, 1)

            act.wait_ge(bias_ready, 1)

            def hi_of_fill(i, r, f):
                slot, kind, part = FILLS[f]
                if kind not in hi_done:
                    return
                acc = dense[f % BANKS]
                count = fill_count(i, f)
                act.wait_ge(filled[kind], count)
                if kind == "qk":
                    c, ring = (slot + 1) % PAIRS, (slot + 1) % 2
                    act.activation(qT[0][:, ring, :], acc[:, 0:N], ACT.Identity, bias=bqs[:, c:c + 1])
                    act.activation(kT[0][:, ring, :], acc[:, N:2 * N], ACT.Identity,
                                   bias=bias_cols[:, DC + c:DC + c + 1]).then_inc(hi_done[kind], 1)
                elif kind == "v":
                    act.activation(v[0][:, r % 2, part, :], acc[:, :], ACT.Copy).then_inc(hi_done[kind], 1)
                elif kind == "ht":
                    act.activation(hT[0][:, 2 * part:2 * part + 2, :].rearrange("p a b -> p (a b)"), acc[:, :],
                                   ACT.Relu).then_inc(hi_done[kind], 1)
                elif kind == "y":
                    act.activation(yT[0][:, 2 * part:2 * part + 2, :].rearrange("p a b -> p (a b)"), acc[:, :],
                                   ACT.Copy).then_inc(hi_done[kind], 1)

            def step(i, r):
                for c in range(PAIRS):
                    g = i * PAIRS + c
                    if pair_exists(g - 1):
                        for e in range(2):
                            act.wait_ge(probT_filled, (g - 1) * 2 + (e + 1))
                            act.activation(pT[0][:, e, :, :].rearrange("p a b -> p (a b)"), probT[e][:, :],
                                           ACT.Copy).then_inc(pT_hi_done, 1)
                    if pair_exists(g):
                        for e in range(2):
                            for t in range(NT):
                                k = e * NT + t
                                act.wait_ge(logit_ready, g * 2 * NT + (k + 1))
                                act.activation(prob[:, e, t, :], logit[:, e, t, :], ACT.Exp, bias=low[:, k:k + 1],
                                               scale=-1.0, accum_out=total[:, k:k + 1]).then_inc(exp_done, 1)
                    for f in fills_of(i, c):
                        hi_of_fill(i, r, f)
                    if c == 2 and exists(i - 1):
                        act.wait_ge(z_ready, i * NT)
                        for t in range(NT):
                            act.activation(h2[0][:, t, :], z[:, t, :], ACT.Relu).then_inc(h2_hi_done, 1)
                    if pair_exists(g - 1):
                        act.wait_ge(attn_filled, g)
                        co = (c - 1) % PAIRS
                        for e in range(2):
                            act.activation(oT[0][e * HD:(e + 1) * HD, co, :], attn[0:HD, e * N:(e + 1) * N],
                                           ACT.Copy).then_inc(oT_hi_done, 1)

            times(act, step)

        @block.vector
        def _(dve):
            def lo(out_lo, acc, hi, inc, op0=ALU.add, scalar=0.0):
                return dve.scalar_tensor_tensor(out=out_lo, in0=acc, scalar=scalar, in1=hi, op0=op0,
                                                op1=ALU.subtract).then_inc(inc, 1)

            dve.wait_ge(bias_turned, 1)
            dve.tensor_copy(bias_cols[:, :], score[1][:, 0:3 * DC]).then_inc(bias_cols_ready, 1)
            dve.wait_ge(bias_cols_ready, 1)
            dve.tensor_scalar(bqs[:, :], bias_cols[:, 0:DC], -SCALE, None, ALU.mult).then_inc(bias_ready, 1)
            dve.tensor_copy(bvb[:, :, :], bias_cols[:, 2 * DC:3 * DC].unsqueeze(2).to_broadcast((P, DC, P))).then_inc(bias_ready, 1)
            for n, (w, _, scale) in enumerate(WEIGHTS):
                dve.wait_ge(w_hi, n + 1)
                dve.scalar_tensor_tensor(out=w[1][:, :, :].rearrange("p a b -> p (a b)"),
                                         in0=stage[:, n % STAGES, :, :].rearrange("p a b -> p (a b)"), scalar=scale,
                                         in1=f32(w[0][:, :, :]).rearrange("p a b -> p (a b)"),
                                         op0=ALU.mult, op1=ALU.subtract).then_inc(w_lo, 1)
                if n == 0:
                    dve.tensor_scalar(mask[:, :, :], adjn[:, :, :], -1.0, 1.0, ALU.mult, ALU.add).then_inc(mask_ready, 1)
                    dve.wait_ge(mask_ready, 1)
                    dve.tensor_scalar(mask[:, :, :], mask[:, :, :], MASK, None, ALU.mult).then_inc(mask_ready, 1)
                    dve.wait_ge(adj_hi, 1)
                    lo(adjT[1][:, :, :].rearrange("p a b -> p (a b)"), score[0][:, :],
                       f32(adjT[0][:, :, :]).rearrange("p a b -> p (a b)"), adj_lo)
                if n == 3:
                    dve.wait_ge(bias_filled, 2)
                    dve.tensor_copy(cbias[:, :], dense[0][:, :]).then_inc(cbias_ready, 1)
                    dve.tensor_copy(obias[:, :], dense[1][:, :]).then_inc(cbias_ready, 1)

            def statistics(src, st, stats, n):
                for t in range(NT):
                    dve.bn_stats(st[:, t, :], src[:, t, :]).then_inc(stats, 1)
                dve.wait_ge(stats, (n + 1) * NT)

            def mean_variance(st, mv, mv_ready):
                for t in range(NT):
                    dve.bn_aggr(mv[:, t, :], st[:, t, :]).then_inc(mv_ready, 1)

            def normalise(dst, src, mv, rs, done):
                for t in range(NT):
                    dve.tensor_scalar(dst[:, t, :], src[:, t, :], mv[:, t, 0:1], rs[:, t:t + 1],
                                      ALU.subtract, ALU.mult).then_inc(done, 1)

            def drain_fill(i, r, f):
                slot, kind, part = FILLS[f]
                acc = dense[f % BANKS]
                count = fill_count(i, f)
                if kind in hi_done:
                    dve.wait_ge(hi_done[kind], count)
                else:
                    dve.wait_ge(filled[kind], count)
                if kind == "qk":
                    c, ring = (slot + 1) % PAIRS, (slot + 1) % 2
                    dve.scalar_tensor_tensor(out=qT[1][:, ring, :], in0=acc[:, 0:N], scalar=bqs[:, c:c + 1],
                                             in1=f32(qT[0][:, ring, :]), op0=ALU.add, op1=ALU.subtract)
                    dve.scalar_tensor_tensor(out=kT[1][:, ring, :], in0=acc[:, N:2 * N], scalar=bias_cols[:, DC + c:DC + c + 1],
                                             in1=f32(kT[0][:, ring, :]), op0=ALU.add, op1=ALU.subtract)\
                       .then_inc(drained[kind], 1)
                elif kind == "v":
                    lo(v[1][:, r % 2, part, :], acc[:, :], f32(v[0][:, r % 2, part, :]), drained[kind])
                elif kind == "ht":
                    lo(hT[1][:, 2 * part:2 * part + 2, :].rearrange("p a b -> p (a b)"), acc[:, :],
                       f32(hT[0][:, 2 * part:2 * part + 2, :]).rearrange("p a b -> p (a b)"), drained[kind], op0=ALU.max)
                elif kind == "y":
                    lo(yT[1][:, 2 * part:2 * part + 2, :].rearrange("p a b -> p (a b)"), acc[:, :],
                       f32(yT[0][:, 2 * part:2 * part + 2, :]).rearrange("p a b -> p (a b)"), drained[kind])
                elif kind == "wo":
                    s = (r - 1) % RING
                    dve.wait_ge(xc_ready, count)
                    dve.tensor_tensor(xr[:, s, part, :], acc[:, :], xr[:, s, part, :], ALU.add).then_inc(drained[kind], 1)
                elif kind == "w1":
                    s = (r - 2) % RING
                    dve.wait_ge(xb_ready, count)
                    dve.tensor_tensor(xr[:, s, part, :], acc[:, :], xr[:, s, part, :], ALU.add).then_inc(drained[kind], 1)

            def step(i, r):
                for c in range(PAIRS):
                    g = i * PAIRS + c
                    if pair_exists(g):
                        dve.wait_ge(mask_ready, 2)
                    if pair_exists(g - 1):
                        for e in range(2):
                            if e == 1 and pair_exists(g):
                                dve.wait_ge(score_filled, g + 1)
                            dve.wait_ge(pT_hi_done, (g - 1) * 2 + (e + 1))
                            lo(pT[1][:, e, :, :].rearrange("p a b -> p (a b)"), probT[e][:, :],
                               f32(pT[0][:, e, :, :]).rearrange("p a b -> p (a b)"), pT_ready)
                    if pair_exists(g):
                        if not pair_exists(g - 1):
                            dve.wait_ge(score_filled, g + 1)
                        for e in range(2):
                            for t in range(NT):
                                k = e * NT + t
                                dve.tensor_tensor_reduce(
                                    out=logit[:, e, t, :], in0=score[e][:, t * N:(t + 1) * N], in1=mask[:, t, :],
                                    scale=1.0, scalar=HUGE, op0=ALU.add, op1=ALU.min,
                                    accum_out=low[:, k:k + 1]).then_inc(logit_ready, 1)
                    fills = fills_of(i, c)
                    for f in fills:
                        if FILLS[f][1] == "qk":
                            drain_fill(i, r, f)
                    if pair_exists(g):
                        dve.wait_ge(exp_done, (g + 1) * 2 * NT)
                        dve.reciprocal(rtotal[:, :], total[:, :]).then_inc(rtotal_ready, 1)
                    if c == 0 and exists(i + 1):
                        n, s = i + 1, (r + 1) % RING
                        dve.wait_ge(x_loaded[s], n * 4 + (16 - 4 * s))
                        statistics(xr[:, s, :, :], st1, stats1, n)
                    if c == 1 and exists(i + 1):
                        s = (r + 1) % RING
                        dve.wait_ge(rs1_ready, i + 2)
                        normalise(h, xr[:, s, :, :], mv1, rs1, h_ready)
                    if c == 2 and exists(i - 1):
                        s = (r - 1) % RING
                        dve.wait_ge(rs2_ready, i)
                        normalise(z, xr[:, s, :, :], mv2, rs2, z_ready)
                    for f in fills:
                        if FILLS[f][1] != "qk":
                            drain_fill(i, r, f)
                    if c == 0 and exists(i + 1):
                        mean_variance(st1, mv1, mv1_ready)
                    if c == 1 and exists(i - 1):
                        s = (r - 1) % RING
                        dve.wait_ge(drained["wo"], i * NT)
                        statistics(xr[:, s, :, :], st2, stats2, i - 1)
                    if c == 2 and exists(i - 1):
                        for t in range(NT):
                            dve.wait_ge(h2_hi_done, (i - 1) * NT + (t + 1))
                            lo(h2[1][:, t, :], z[:, t, :], f32(h2[0][:, t, :]), h2_ready, op0=ALU.max)
                    if pair_exists(g - 1):
                        co = (c - 1) % PAIRS
                        dve.wait_ge(oT_hi_done, g * 2)
                        for e in range(2):
                            lo(oT[1][e * HD:(e + 1) * HD, co, :], attn[0:HD, e * N:(e + 1) * N],
                               f32(oT[0][e * HD:(e + 1) * HD, co, :]), oT_ready)
                    if c == 1 and exists(i - 1):
                        mean_variance(st2, mv2, mv2_ready)

            times(dve, step)

        @block.tensor
        def _(pe):
            def three(acc, a, b, first, last):
                pe.matmul(acc, a[0], b[0], start=first, stop=False)
                pe.matmul(acc, a[0], b[1], start=False, stop=False)
                return pe.matmul(acc, a[1], b[0], start=False, stop=last)

            def half(pair, *index):
                return pair[0][index], pair[1][index]

            ALL = slice(None)

            def cols(k, width=P):
                return slice(k * width, (k + 1) * width)

            pe.wait_ge(adj_loaded, 16)
            pe.wait_ge(ident_ready, 2)
            for t in range(NT):
                for m in range(NT):
                    mm = pe.transpose(score[0][:, m * N + t * P:m * N + (t + 1) * P], adjn[:, t, cols(m)], ident[:, :])
            mm.then_inc(adj_turned, 1)
            pe.wait_ge(bias_loaded, 5 * 16)
            pe.transpose(score[1][:, 0:3 * DC], bias_rows[:, :], ident[0:3 * DC, 0:3 * DC]).then_inc(bias_turned, 1)
            pe.wait_ge(ones_ready, 1)
            pe.matmul(dense[1][:, :], ones[:, :], rows[:, 1, :], start=True, stop=True).then_inc(bias_filled, 1)
            pe.matmul(dense[0][:, :], ones[:, :], rows[:, 0, :], start=True, stop=False)
            pe.wait_ge(bias_ready, 2)
            pe.wait_ge(w_loaded[3], 16)
            for c in range(DC):
                mm = pe.matmul(dense[0][:, :], bvb[:, c, :], stage[:, 3 % STAGES, c, :], start=False, stop=(c == DC - 1))
            mm.then_inc(bias_filled, 1)
            pe.wait_ge(cbias_ready, 2)

            def fill(i, r, f):
                slot, kind, part = FILLS[f]
                acc = dense[f % BANKS]
                before = bank_user_before(i, f)
                if before:
                    pe.wait_ge(drained[before[0]], before[1])
                static = isinstance(i, int)
                if kind == "qk":
                    if static and i == -1:
                        pe.wait_ge(w_lo, 2)
                    if slot == 3:
                        pe.wait_ge(drained["ht"], (i + 2) * 2)
                    c = (slot + 1) % PAIRS
                    for w, at in ((wq, 0), (wk, N)):
                        for k in range(DC):
                            mm = three(acc[:, at:at + N], half(w, ALL, k, cols(c)), half(hT, ALL, k, ALL),
                                       k == 0, k == DC - 1)
                elif kind == "v":
                    if static and i == 0:
                        pe.wait_ge(w_lo, 3)
                    for k in range(DC):
                        mm = three(acc[:, :], half(hT, ALL, k, cols(part)), half(wv, ALL, k, ALL), k == 0, k == DC - 1)
                elif kind == "ht":
                    if part == 0:
                        pe.wait_ge(h_ready, (i + 2) * NT)
                    for k in range(2):
                        for t in range(NT):
                            mm = pe.transpose(acc[:, k * N + t * P:k * N + (t + 1) * P],
                                              h[:, t, cols(2 * part + k)], ident[:, :])
                elif kind == "wo":
                    if part == 0:
                        pe.wait_ge(oT_ready, i * H)
                    if static and i == 1:
                        pe.wait_ge(w_lo, 4)
                    for k in range(DC):
                        mm = three(acc[:, :], half(oT, ALL, k, cols(part)), half(wo, ALL, k, ALL), k == 0, k == DC - 1)
                elif kind == "y":
                    if part == 0:
                        pe.wait_ge(h2_ready, i * NT)
                    if static and i == 1:
                        pe.wait_ge(adj_lo, 1)
                    for k in range(2):
                        for t in range(NT):
                            mm = three(acc[:, k * N:(k + 1) * N], half(h2, ALL, t, cols(2 * part + k)),
                                       half(adjT, ALL, t, ALL), t == 0, t == NT - 1)
                elif kind == "w1":
                    if part == 0:
                        pe.wait_ge(drained["y"], (i - 1) * 2)
                    if static and i == 2:
                        pe.wait_ge(w_lo, 5)
                    for k in range(DC):
                        mm = three(acc[:, :], half(yT, ALL, k, cols(part)), half(w1, ALL, k, ALL), k == 0, k == DC - 1)
                mm.then_inc(filled[kind], 1)

            def step(i, r):
                for c in range(PAIRS):
                    g = i * PAIRS + c
                    if pair_exists(g - 1):
                        for e in range(2):
                            if pair_exists(g - 2):
                                pe.wait_ge(pT_ready, (g - 2) * 2 + (e + 1))
                            pe.wait_ge(prob_ready, (g - 1) * 2 + (e + 1))
                            for t in range(NT):
                                for m in range(NT):
                                    mm = pe.transpose(probT[e][:, m * N + t * P:m * N + (t + 1) * P],
                                                      prob[:, e, t, cols(m)], ident[:, :])
                            mm.then_inc(probT_filled, 1)
                    if pair_exists(g):
                        pe.wait_ge(drained["qk"], g + 1)
                        if pair_exists(g - 1):
                            pe.wait_ge(logit_ready, g * 2 * NT)
                        else:
                            pe.wait_ge(adj_lo, 1)
                        for t in range(NT):
                            for n, (qa, ka) in enumerate(((0, 0), (0, 1), (1, 0))):
                                for e in range(2):
                                    rowsl = slice(e * HD, (e + 1) * HD)
                                    mm = pe.matmul(score[e][:, t * N:(t + 1) * N], qT[qa][rowsl, c % 2, cols(t)],
                                                   kT[ka][rowsl, c % 2, :], start=(n == 0), stop=(n == 2))
                        mm.then_inc(score_filled, 1)
                    for f in fills_of(i, c):
                        fill(i, r, f)
                    if pair_exists(g - 1):
                        if pair_exists(g - 2):
                            pe.wait_ge(oT_ready, (g - 1) * 2)
                        co = (c - 1) % PAIRS
                        ring = (r if c else r - 1) % 2
                        if c == 1:
                            pe.wait_ge(drained["v"], i * NT + NT)
                        for e in range(2):
                            pe.wait_ge(pT_ready, (g - 1) * 2 + (e + 1))
                            for t in range(NT):
                                mm = three(attn[0:HD, e * N:(e + 1) * N], half(v, ALL, ring, t, cols(2 * co + e, HD)),
                                           half(pT, ALL, e, t, ALL), t == 0, t == NT - 1)
                        mm.then_inc(attn_filled, 1)

            times(pe, step)


_INS = ["x", "adj", "L0_gnn_Wq", "L0_gnn_bq", "L0_gnn_Wk", "L0_gnn_bk", "L0_gnn_Wv", "L0_gnn_bv",
        "L0_gnn_Wo", "L0_gnn_bo", "L1_gnn_weight", "L1_gnn_bias"]


def kernel(**inputs):
    import numpy as _np
    import concourse.bacc as _bacc
    from concourse import mybir as _mybir
    from concourse.bass_utils import run_bass_kernel_spmd as _run

    nc = _bacc.Bacc("TRN2", target_bir_lowering=False, num_devices=1)
    arrays, args = {}, []
    for name in _INS:
        a = _np.ascontiguousarray(inputs[name])
        arrays[f"in_{name}_dram"] = a
        args.append(nc.dram_tensor(f"in_{name}_dram", a.shape, _mybir.dt.from_np(a.dtype), kind="ExternalInput").ap())
    shape = tuple(inputs["x"].shape)
    args.append(nc.dram_tensor("out_0_dram", shape, _mybir.dt.float32, kind="ExternalOutput").ap())
    adjacency_layers(nc, *args)
    r = _run(nc, [arrays], core_ids=[0])
    return r.results[0]["out_0_dram"]
```

```python
from contextlib import ExitStack

import concourse.bass as bass
from concourse import mybir

F32 = mybir.dt.float32
F32R = mybir.dt.float32r
ALU = mybir.AluOpType
ACT = mybir.ActivationFunctionType

P = 128
EPS = 1e-5
MASK = 1e9
HUGE = 3.0e38


def adjacency_layers(nc, x, adj, Wq, bq, Wk, bk, Wv, bv, Wo, bo, W1, b1, out):
    NB, N, D = x.shape
    H = 8
    HD = D // H
    NT = N // P
    DC = D // P
    PAIRS = H // 2
    RING = 4
    SCALE = 1.0 / HD ** 0.5
    assert HD * 2 == P and PAIRS == DC and N * 2 == D and SCALE == 0.125

    FIRST, END = 2, NB - 2
    assert (END - FIRST) % RING == 0

    FILLS = [
        (0, "qk", 0), (0, "v", 0), (0, "v", 1),
        (1, "qk", 0), (1, "wo", 0), (1, "wo", 1),
        (2, "qk", 0), (2, "w1", 0), (2, "ht", 0), (2, "ht", 1),
        (3, "w1", 1), (3, "qk", 0), (3, "y", 0), (3, "y", 1),
    ]
    LATE = [(2, "ht", 1)]
    LAG = {"v": 0, "wo": 1, "ht": -1, "w1": 2, "y": 1}
    BANKS = 3

    def exists(batch):
        return not isinstance(batch, int) or 0 <= batch < NB

    def pair_exists(g):
        return not isinstance(g, int) or 0 <= g < NB * PAIRS

    def fill_count(i, f):
        slot, kind, part = FILLS[f]
        if kind == "qk":
            g = i * PAIRS + (slot + 1)
            return g + 1 if pair_exists(g) else None
        n = i - LAG[kind]
        return n * 2 + (part + 1) if exists(n) else None

    def fills_of(i, slot, late=False):
        return [f for f, fill in enumerate(FILLS)
                if fill[0] == slot and (fill in LATE) == late and fill_count(i, f) is not None]

    def bank_user_before(i, f):
        bank, k, t = f % BANKS, f, i
        while True:
            k -= 1
            if k < 0:
                k, t = len(FILLS) - 1, t - 1
                if isinstance(t, int) and t < -1:
                    return None
            if k % BANKS == bank and fill_count(t, k) is not None:
                return FILLS[k][1], fill_count(t, k)

    def times(eng, step):
        for i in range(-1, FIRST):
            step(i, i % RING)
        with eng.Fori(0, (END - FIRST) // RING) as m:
            for j in range(RING):
                step(m * RING + (FIRST + j), (FIRST + j) % RING)
        for i in range(END, NB + 2):
            step(i, i % RING)

    with ExitStack() as ctx:
        def sb(name, shape, dt=F32):
            return ctx.enter_context(nc.sbuf_tensor(name, shape, dt))

        def sem(name):
            return ctx.enter_context(nc.semaphore(name))

        def split_pair(name, shape):
            return sb(name + "_hi", shape, F32R), sb(name + "_lo", shape, F32R)

        wq, wk, wv, wo, w1 = (split_pair(n, [P, DC, D]) for n in ("wq", "wk", "wv", "wo", "w1"))
        adjT = split_pair("adjT", [P, NT, N])
        mask = sb("mask", [P, NT, N])
        cbias = sb("cbias", [P, D])
        obias = sb("obias", [P, D])
        ident = sb("ident", [P, P])
        stage = sb("stage", [P, 2, DC, D])
        bias_rows = sb("bias_rows", [3 * DC, P])
        bias_cols = sb("bias_cols", [P, 3 * DC])
        bqs = sb("bqs", [P, DC])
        ones = sb("ones", [1, P])
        nhalf, eps = sb("nhalf", [P, NT]), sb("eps", [P, NT])

        xr = sb("xr", [P, RING, NT, D])
        h = sb("h", [P, NT, D])
        hT = split_pair("hT", [P, DC, N])
        qT = split_pair("qT", [P, 2, N])
        kT = split_pair("kT", [P, 2, N])
        v = sb("v", [P, 2, NT, H, 2, HD], F32R)
        logit = sb("logit", [P, 2, NT, N])
        adjn = logit[:, 0, :, :]
        low = sb("low", [P, 2 * NT])
        prob = sb("prob", [P, 2, NT, N])
        b1_row = prob[0:1, 0, :, :].rearrange("p a b -> p (a b)")
        total = sb("total", [P, 2 * NT])
        rtotal = sb("rtotal", [P, 2 * NT])
        pT = split_pair("pT", [P, 2, NT, N])
        oT = split_pair("oT", [P, DC, N])
        omain, orest = sb("omain", [P, N]), sb("orest", [P, N])
        z = sb("z", [P, NT, D])
        bvb = z[:, 0, :].rearrange("p (c n) -> p c n", c=DC)
        bo_row = z[0:1, 1, :]
        h2 = split_pair("h2", [P, NT, D])
        yT = split_pair("yT", [P, DC, N])
        st1 = sb("st1", [P, NT, 6]); mv1 = sb("mv1", [P, NT, 2]); rs1 = sb("rs1", [P, NT]); ve1 = sb("ve1", [P, NT])
        st2 = sb("st2", [P, NT, 6]); mv2 = sb("mv2", [P, NT, 2]); rs2 = sb("rs2", [P, NT]); ve2 = sb("ve2", [P, NT])

        def bank(name):
            return ctx.enter_context(nc.psum_tensor(name, [P, 512], F32))
        dense = [bank(f"dense{b}") for b in range(BANKS)]
        score = [bank(f"score{e}") for e in range(2)]
        probT = [bank(f"probT{e}") for e in range(2)]
        attn = bank("attn")

        x_loaded = [sem(f"x_loaded{r}") for r in range(RING)]
        x_stored = [sem(f"x_stored{r}") for r in range(RING)]
        w_loaded = [sem(f"w_loaded{n}") for n in range(5)]
        adj_loaded, bias_loaded = sem("adj_loaded"), sem("bias_loaded")
        ident_ready, ones_ready, powers_ready = sem("ident_ready"), sem("ones_ready"), sem("powers_ready")
        w_hi, w_lo = sem("w_hi"), sem("w_lo")
        adj_turned, adj_hi, adj_lo = sem("adj_turned"), sem("adj_hi"), sem("adj_lo")
        mask_ready, bias_ready = sem("mask_ready"), sem("bias_ready")
        bias_turned, bias_cols_ready = sem("bias_turned"), sem("bias_cols_ready")
        bias_filled, cbias_ready = sem("bias_filled"), sem("cbias_ready")
        KINDS = ("qk", "v", "wo", "ht", "w1", "y")
        filled = {k: sem(f"{k}_filled") for k in KINDS}
        hi_done = {k: sem(f"{k}_hi_done") for k in ("qk", "v", "ht", "y")}
        drained = {k: sem(f"{k}_drained") for k in KINDS}
        score_filled, logit_ready, exp_done = sem("score_filled"), sem("logit_ready"), sem("exp_done")
        rtotal_ready, prob_ready = sem("rtotal_ready"), sem("prob_ready")
        probT_filled, pT_hi_done, pT_ready = sem("probT_filled"), sem("pT_hi_done"), sem("pT_ready")
        attn_filled, orest_ready, omain_ready = sem("attn_filled"), sem("orest_ready"), sem("omain_ready")
        oT_hi_done, oT_ready = sem("oT_hi_done"), sem("oT_ready")
        stats1, mv1_ready, rs1_ready, h_ready, xc_ready = (sem(n) for n in ("stats1", "mv1_ready", "rs1_ready", "h_ready", "xc_ready"))
        stats2, mv2_ready, rs2_ready, z_ready, xb_ready = (sem(n) for n in ("stats2", "mv2_ready", "rs2_ready", "z_ready", "xb_ready"))
        var1_ready, var2_ready = sem("var1_ready"), sem("var2_ready")
        h2_hi_done, h2_ready = sem("h2_hi_done"), sem("h2_ready")

        staged = [stage[:, 0, :, :], stage[:, 1, :, :],
                  xr[:, 2:4, :, :].rearrange("p a b d -> p (a b) d"), stage[:, 0, :, :], stage[:, 1, :, :]]

        def f32(ap):
            return ap.bitcast(F32)

        WEIGHTS = [(wq, Wq, -SCALE), (wk, Wk, 1.0), (wv, Wv, 1.0), (wo, Wo, 1.0), (w1, W1, 1.0)]

        block = ctx.enter_context(nc.Block())

        @block.sync
        def _(sp):
            def load_x(b, r):
                sp.dma_start(xr[:, r, :, :], x[b].rearrange("(t p) d -> p t d", p=P)).then_inc(x_loaded[r], 16)

            def load_w(n):
                sp.dma_start(staged[n], WEIGHTS[n][1].rearrange("(c p) n -> p c n", p=P)).then_inc(w_loaded[n], 16)

            load_x(0, 0)
            load_w(0)
            load_w(1)
            sp.dma_start(adjn[:, :, :], adj.rearrange("(t p) m -> p t m", p=P)).then_inc(adj_loaded, 16)
            load_w(2)
            load_x(1, 1)
            for n in (3, 4):
                sp.wait_ge(w_lo, n - 2)
                load_w(n)
            sp.wait_ge(w_lo, 3)
            load_x(2, 2)
            load_x(3, 3)

            def step(i, r):
                if exists(i - 2):
                    sp.wait_ge(drained["w1"], (i - 2) * NT + NT)
                    s = (r - 2) % RING
                    sp.dma_start(out[i - 2].rearrange("(t p) d -> p t d", p=P), xr[:, s, :, :]).then_inc(x_stored[s], 16)
                    if exists(i + 2):
                        sp.wait_ge(x_stored[s], (i - 2) * 4 + (16 - 4 * s))
                        load_x(i + 2, s)

            times(sp, step)
            for s in range(RING):
                sp.wait_ge(x_stored[s], 16 * (NB // RING))

        @block.gpsimd
        def _(pool):
            for n, b in enumerate((bq, bk, bv)):
                pool.dma_start(bias_rows[n * DC:(n + 1) * DC, :], b.rearrange("(c p) -> c p", p=P)).then_inc(bias_loaded, 16)
            pool.dma_start(bo_row, bo.rearrange("(a n) -> a n", a=1)).then_inc(bias_loaded, 16)
            pool.dma_start(b1_row, b1.rearrange("(a n) -> a n", a=1)).then_inc(bias_loaded, 16)
            pool.memset(nhalf[:, :], -0.5).then_inc(powers_ready, 1)
            pool.memset(eps[:, :], EPS).then_inc(powers_ready, 1)
            pool.memset(ident[:, :], 0.0).then_inc(ident_ready, 1)
            pool.memset(ones[:, :], 1.0).then_inc(ones_ready, 1)
            pool.wait_ge(ident_ready, 1)
            pool.affine_select(out=ident[:, :], in_=ident[:, :], compare_op=ALU.not_equal, fill=1.0,
                               base=0, pattern=[[-1, P]], channel_multiplier=1).then_inc(ident_ready, 1)
            pool.wait_ge(powers_ready, 2)

            def norm_scale(mv, mv_ready, ve, var_ready, rs, rs_ready, n):
                pool.wait_ge(mv_ready, (n + 1) * NT)
                pool.tensor_tensor(ve[:, :], mv[:, :, 1], eps[:, :], ALU.add).then_inc(var_ready, 1)
                pool.wait_ge(var_ready, n + 1)
                pool.tensor_tensor(rs[:, :], ve[:, :], nhalf[:, :], ALU.pow).then_inc(rs_ready, 1)

            def step(i, r):
                for c in range(PAIRS):
                    g = i * PAIRS + c
                    if pair_exists(g - 2):
                        pool.wait_ge(oT_hi_done, g - 1)
                        co = (c - 2) % PAIRS
                        pool.tensor_tensor(oT[1][:, co, :], omain[:, :], f32(oT[0][:, co, :]), ALU.subtract).then_inc(oT_ready, 1)
                    if c == 2 and exists(i - 1):
                        norm_scale(mv2, mv2_ready, ve2, var2_ready, rs2, rs2_ready, i - 1)
                    if pair_exists(g):
                        for e in range(2):
                            if e == 0:
                                pool.wait_ge(rtotal_ready, g + 1)
                            pool.tensor_tensor(
                                prob[:, e, :, :], prob[:, e, :, :],
                                rtotal[:, e * NT:(e + 1) * NT].unsqueeze(2).to_broadcast((P, NT, N)),
                                ALU.mult).then_inc(prob_ready, 1)
                    if c == 0 and exists(i + 1):
                        norm_scale(mv1, mv1_ready, ve1, var1_ready, rs1, rs1_ready, i + 1)
                    if c == 0 and exists(i - 1):
                        pool.wait_ge(h_ready, i * NT)
                        if isinstance(i, int) and i == 1:
                            pool.wait_ge(cbias_ready, 2)
                        s = (r - 1) % RING
                        for t in range(NT):
                            pool.tensor_tensor(xr[:, s, t, :], xr[:, s, t, :], cbias[:, :], ALU.add).then_inc(xc_ready, 1)
                    if c == 2 and exists(i - 1):
                        pool.wait_ge(z_ready, i * NT)
                        s = (r - 1) % RING
                        for t in range(NT):
                            pool.tensor_tensor(xr[:, s, t, :], xr[:, s, t, :], obias[:, :], ALU.add).then_inc(xb_ready, 1)

            times(pool, step)

        @block.scalar
        def _(act):
            def weight_hi(n):
                w, _, scale = WEIGHTS[n]
                act.wait_ge(w_loaded[n], 16)
                act.activation(w[0][:, :, :], staged[n], ACT.Copy, scale=scale).then_inc(w_hi, 1)

            def setup(i, c):
                if (i, c) == (-1, 3):
                    weight_hi(0)
                    weight_hi(1)
                    act.wait_ge(bias_ready, 1)
                if (i, c) == (0, 0):
                    act.wait_ge(adj_turned, 1)
                    act.activation(adjT[0][:, :, :].rearrange("p a b -> p (a b)"), score[0][:, :], ACT.Copy).then_inc(adj_hi, 1)
                    weight_hi(2)
                if (i, c) == (1, 0):
                    weight_hi(3)
                if (i, c) == (1, 1):
                    weight_hi(4)

            def hi_of_fill(i, r, f):
                slot, kind, part = FILLS[f]
                if kind not in hi_done:
                    return
                acc = dense[f % BANKS]
                count = fill_count(i, f)
                act.wait_ge(filled[kind], count)
                if kind == "qk":
                    c, ring = (slot + 1) % PAIRS, (slot + 1) % 2
                    act.activation(qT[0][:, ring, :], acc[:, 0:N], ACT.Identity, bias=bqs[:, c:c + 1])
                    act.activation(kT[0][:, ring, :], acc[:, N:2 * N], ACT.Identity,
                                   bias=bias_cols[:, DC + c:DC + c + 1]).then_inc(hi_done[kind], 1)
                elif kind == "v":
                    act.activation(v[:, r % 2, part, :, 0, :], acc[:, :].rearrange("p (h d) -> p h d", h=H), ACT.Copy).then_inc(hi_done[kind], 1)
                elif kind == "ht":
                    act.activation(hT[0][:, 2 * part:2 * part + 2, :].rearrange("p a b -> p (a b)"), acc[:, :],
                                   ACT.Relu).then_inc(hi_done[kind], 1)
                elif kind == "y":
                    act.activation(yT[0][:, 2 * part:2 * part + 2, :].rearrange("p a b -> p (a b)"), acc[:, :],
                                   ACT.Copy).then_inc(hi_done[kind], 1)

            def step(i, r):
                for c in range(PAIRS):
                    g = i * PAIRS + c
                    if isinstance(i, int):
                        setup(i, c)
                    if pair_exists(g - 1):
                        for e in range(2):
                            act.wait_ge(probT_filled, (g - 1) * 2 + (e + 1))
                            act.activation(pT[0][:, e, :, :].rearrange("p a b -> p (a b)"), probT[e][:, :],
                                           ACT.Copy).then_inc(pT_hi_done, 1)
                    if pair_exists(g - 2):
                        act.wait_ge(omain_ready, (g - 1) * 2)
                        act.activation(oT[0][:, (c - 2) % PAIRS, :], omain[:, :], ACT.Copy).then_inc(oT_hi_done, 1)
                    if pair_exists(g):
                        for e in range(2):
                            for t in range(NT):
                                k = e * NT + t
                                act.wait_ge(logit_ready, g * 2 * NT + (k + 1))
                                act.activation(prob[:, e, t, :], logit[:, e, t, :], ACT.Exp, bias=low[:, k:k + 1],
                                               scale=-1.0, accum_out=total[:, k:k + 1]).then_inc(exp_done, 1)
                    for f in fills_of(i, c):
                        hi_of_fill(i, r, f)
                    if c == 2 and exists(i - 1):
                        act.wait_ge(z_ready, i * NT)
                        for t in range(NT):
                            act.activation(h2[0][:, t, :], z[:, t, :], ACT.Relu).then_inc(h2_hi_done, 1)
                    if pair_exists(g - 1):
                        act.wait_ge(attn_filled, g)
                        for e in range(2):
                            act.activation(orest[e * HD:(e + 1) * HD, :], attn[HD:P, e * N:(e + 1) * N],
                                           ACT.Copy).then_inc(orest_ready, 1)
                    for f in fills_of(i, c, late=True):
                        hi_of_fill(i, r, f)

            times(act, step)

        @block.vector
        def _(dve):
            def lo(out_lo, acc, hi, inc, op0=ALU.add, scalar=0.0):
                return dve.scalar_tensor_tensor(out=out_lo, in0=acc, scalar=scalar, in1=hi, op0=op0,
                                                op1=ALU.subtract).then_inc(inc, 1)

            def weight_lo(n):
                w, _, scale = WEIGHTS[n]
                dve.wait_ge(w_hi, n + 1)
                dve.scalar_tensor_tensor(out=w[1][:, :, :], in0=staged[n], scalar=scale, in1=f32(w[0][:, :, :]),
                                         op0=ALU.mult, op1=ALU.subtract).then_inc(w_lo, 1)

            def setup(i, c):
                if (i, c) == (-1, 2):
                    dve.wait_ge(bias_turned, 1)
                    dve.tensor_copy(bias_cols[:, :], score[1][:, 0:3 * DC]).then_inc(bias_cols_ready, 1)
                    dve.wait_ge(bias_cols_ready, 1)
                    dve.tensor_scalar(bqs[:, :], bias_cols[:, 0:DC], -SCALE, None, ALU.mult).then_inc(bias_ready, 1)
                    dve.tensor_copy(bvb[:, :, :], bias_cols[:, 2 * DC:3 * DC].unsqueeze(2)
                                    .to_broadcast((P, DC, P))).then_inc(bias_ready, 1)
                    dve.wait_ge(bias_filled, 1)
                    dve.tensor_copy(obias[:, :], dense[1][:, :]).then_inc(cbias_ready, 1)
                if (i, c) == (-1, 3):
                    weight_lo(0)
                    weight_lo(1)
                if (i, c) == (0, 0):
                    dve.wait_ge(adj_loaded, 16)
                    dve.tensor_scalar(mask[:, :, :], adjn[:, :, :], -1.0, 1.0, ALU.mult, ALU.add).then_inc(mask_ready, 1)
                    dve.wait_ge(mask_ready, 1)
                    dve.tensor_scalar(mask[:, :, :], mask[:, :, :], MASK, None, ALU.mult).then_inc(mask_ready, 1)
                    dve.wait_ge(adj_hi, 1)
                    lo(adjT[1][:, :, :].rearrange("p a b -> p (a b)"), score[0][:, :],
                       f32(adjT[0][:, :, :]).rearrange("p a b -> p (a b)"), adj_lo)
                    weight_lo(2)
                if (i, c) == (1, 0):
                    dve.wait_ge(bias_filled, 2)
                    dve.tensor_copy(cbias[:, :], attn[:, :]).then_inc(cbias_ready, 1)
                    weight_lo(3)
                if (i, c) == (1, 1):
                    weight_lo(4)

            def statistics(src, st, stats, n):
                for t in range(NT):
                    dve.bn_stats(st[:, t, :], src[:, t, :]).then_inc(stats, 1)
                dve.wait_ge(stats, (n + 1) * NT)

            def mean_variance(st, mv, mv_ready):
                for t in range(NT):
                    dve.bn_aggr(mv[:, t, :], st[:, t, :]).then_inc(mv_ready, 1)

            def normalise(dst, src, mv, rs, done):
                for t in range(NT):
                    dve.tensor_scalar(dst[:, t, :], src[:, t, :], mv[:, t, 0:1], rs[:, t:t + 1],
                                      ALU.subtract, ALU.mult).then_inc(done, 1)

            def drain_fill(i, r, f):
                slot, kind, part = FILLS[f]
                acc = dense[f % BANKS]
                count = fill_count(i, f)
                if kind in hi_done:
                    dve.wait_ge(hi_done[kind], count)
                else:
                    dve.wait_ge(filled[kind], count)
                if kind == "qk":
                    c, ring = (slot + 1) % PAIRS, (slot + 1) % 2
                    dve.scalar_tensor_tensor(out=qT[1][:, ring, :], in0=acc[:, 0:N], scalar=bqs[:, c:c + 1],
                                             in1=f32(qT[0][:, ring, :]), op0=ALU.add, op1=ALU.subtract)
                    dve.scalar_tensor_tensor(out=kT[1][:, ring, :], in0=acc[:, N:2 * N], scalar=bias_cols[:, DC + c:DC + c + 1],
                                             in1=f32(kT[0][:, ring, :]), op0=ALU.add, op1=ALU.subtract)\
                       .then_inc(drained[kind], 1)
                elif kind == "v":
                    lo(v[:, r % 2, part, :, 1, :], acc[:, :].rearrange("p (h d) -> p h d", h=H),
                       f32(v[:, r % 2, part, :, 0, :]), drained[kind])
                elif kind == "ht":
                    lo(hT[1][:, 2 * part:2 * part + 2, :].rearrange("p a b -> p (a b)"), acc[:, :],
                       f32(hT[0][:, 2 * part:2 * part + 2, :]).rearrange("p a b -> p (a b)"), drained[kind], op0=ALU.max)
                elif kind == "y":
                    lo(yT[1][:, 2 * part:2 * part + 2, :].rearrange("p a b -> p (a b)"), acc[:, :],
                       f32(yT[0][:, 2 * part:2 * part + 2, :]).rearrange("p a b -> p (a b)"), drained[kind])
                elif kind == "wo":
                    s = (r - 1) % RING
                    dve.wait_ge(xc_ready, count)
                    dve.tensor_tensor(xr[:, s, part, :], acc[:, :], xr[:, s, part, :], ALU.add).then_inc(drained[kind], 1)
                elif kind == "w1":
                    s = (r - 2) % RING
                    dve.wait_ge(xb_ready, count)
                    dve.tensor_tensor(xr[:, s, part, :], acc[:, :], xr[:, s, part, :], ALU.add).then_inc(drained[kind], 1)

            def step(i, r):
                for c in range(PAIRS):
                    g = i * PAIRS + c
                    if isinstance(i, int):
                        setup(i, c)
                    if pair_exists(g):
                        dve.wait_ge(mask_ready, 2)
                    if pair_exists(g - 1):
                        for e in range(2):
                            if e == 1 and pair_exists(g):
                                dve.wait_ge(score_filled, g + 1)
                            dve.wait_ge(pT_hi_done, (g - 1) * 2 + (e + 1))
                            lo(pT[1][:, e, :, :].rearrange("p a b -> p (a b)"), probT[e][:, :],
                               f32(pT[0][:, e, :, :]).rearrange("p a b -> p (a b)"), pT_ready)
                    if c == 2 and exists(i - 1):
                        mean_variance(st2, mv2, mv2_ready)
                    if pair_exists(g):
                        if not pair_exists(g - 1):
                            dve.wait_ge(score_filled, g + 1)
                        for e in range(2):
                            for t in range(NT):
                                k = e * NT + t
                                dve.tensor_tensor_reduce(
                                    out=logit[:, e, t, :], in0=score[e][:, t * N:(t + 1) * N], in1=mask[:, t, :],
                                    scale=1.0, scalar=HUGE, op0=ALU.add, op1=ALU.min,
                                    accum_out=low[:, k:k + 1]).then_inc(logit_ready, 1)
                    fills = fills_of(i, c)
                    if pair_exists(g):
                        dve.wait_ge(exp_done, (g + 1) * 2 * NT)
                        dve.reciprocal(rtotal[:, :], total[:, :]).then_inc(rtotal_ready, 1)
                    first = next((k + 1 for k, f in enumerate(fills) if FILLS[f][1] == "qk"), 0)
                    for f in fills[:first]:
                        drain_fill(i, r, f)
                    if c == 0 and exists(i + 1):
                        n, s = i + 1, (r + 1) % RING
                        dve.wait_ge(x_loaded[s], n * 4 + (16 - 4 * s))
                        statistics(xr[:, s, :, :], st1, stats1, n)
                    if c == 1 and exists(i + 1):
                        s = (r + 1) % RING
                        dve.wait_ge(rs1_ready, i + 2)
                        normalise(h, xr[:, s, :, :], mv1, rs1, h_ready)
                    if c == 2 and exists(i - 1):
                        s = (r - 1) % RING
                        dve.wait_ge(rs2_ready, i)
                        normalise(z, xr[:, s, :, :], mv2, rs2, z_ready)
                    for f in fills[first:]:
                        drain_fill(i, r, f)
                    if c == 0 and exists(i + 1):
                        mean_variance(st1, mv1, mv1_ready)
                    if c == 2 and exists(i - 1):
                        for t in range(NT):
                            dve.wait_ge(h2_hi_done, (i - 1) * NT + (t + 1))
                            lo(h2[1][:, t, :], z[:, t, :], f32(h2[0][:, t, :]), h2_ready, op0=ALU.max)
                    if pair_exists(g - 1):
                        dve.wait_ge(orest_ready, g * 2)
                        if pair_exists(g - 2):
                            dve.wait_ge(oT_ready, g - 1)
                        for e in range(2):
                            own = slice(e * HD, (e + 1) * HD)
                            dve.tensor_tensor(omain[own, :], attn[0:HD, e * N:(e + 1) * N], orest[own, :],
                                              ALU.add).then_inc(omain_ready, 1)
                    for f in fills_of(i, c, late=True):
                        drain_fill(i, r, f)
                    if c == 1 and exists(i - 1):
                        s = (r - 1) % RING
                        dve.wait_ge(drained["wo"], i * NT)
                        statistics(xr[:, s, :, :], st2, stats2, i - 1)

            times(dve, step)

        @block.tensor
        def _(pe):
            def three(acc, a, b, first, last):
                pe.matmul(acc, a[0], b[0], start=first, stop=False)
                pe.matmul(acc, a[0], b[1], start=False, stop=False)
                return pe.matmul(acc, a[1], b[0], start=False, stop=last)

            def half(pair, *index):
                return pair[0][index], pair[1][index]

            ALL = slice(None)

            def cols(k, width=P):
                return slice(k * width, (k + 1) * width)

            def setup(i, c):
                if (i, c) == (-1, 2):
                    pe.wait_ge(ident_ready, 2)
                    pe.wait_ge(bias_loaded, 5 * 16)
                    pe.transpose(score[1][:, 0:3 * DC], bias_rows[:, :], ident[0:3 * DC, 0:3 * DC]).then_inc(bias_turned, 1)
                    pe.wait_ge(ones_ready, 1)
                    pe.matmul(dense[1][:, :], ones[:, :], b1_row, start=True, stop=True).then_inc(bias_filled, 1)
                if (i, c) == (-1, 3):
                    pe.wait_ge(adj_loaded, 16)
                    for t in range(NT):
                        for m in range(NT):
                            mm = pe.transpose(score[0][:, m * N + t * P:m * N + (t + 1) * P], adjn[:, t, cols(m)], ident[:, :])
                    mm.then_inc(adj_turned, 1)
                    pe.wait_ge(cbias_ready, 1)
                if (i, c) == (1, 0):
                    pe.wait_ge(bias_ready, 2)
                    pe.wait_ge(w_loaded[3], 16)
                    pe.wait_ge(omain_ready, 2 * (PAIRS - 1))
                    pe.matmul(attn[:, :], ones[:, :], bo_row, start=True, stop=False)
                    for k in range(DC):
                        mm = pe.matmul(attn[:, :], bvb[:, k, :], staged[3][:, k, :], start=False, stop=(k == DC - 1))
                    mm.then_inc(bias_filled, 1)

            def fill(i, r, f):
                slot, kind, part = FILLS[f]
                acc = dense[f % BANKS]
                before = bank_user_before(i, f)
                if before:
                    pe.wait_ge(drained[before[0]], before[1])
                static = isinstance(i, int)
                if kind == "qk":
                    if static and i == -1:
                        pe.wait_ge(w_lo, 2)
                    if slot == 3:
                        pe.wait_ge(drained["ht"], (i + 2) * 2)
                    c = (slot + 1) % PAIRS
                    for w, at in ((wq, 0), (wk, N)):
                        for k in range(DC):
                            mm = three(acc[:, at:at + N], half(w, ALL, k, cols(c)), half(hT, ALL, k, ALL),
                                       k == 0, k == DC - 1)
                elif kind == "v":
                    if static and i == 0:
                        pe.wait_ge(w_lo, 3)
                    for k in range(DC):
                        mm = three(acc[:, :], half(hT, ALL, k, cols(part)), half(wv, ALL, k, ALL), k == 0, k == DC - 1)
                elif kind == "ht":
                    if part == 0:
                        pe.wait_ge(h_ready, (i + 2) * NT)
                    for k in range(2):
                        for t in range(NT):
                            mm = pe.transpose(acc[:, k * N + t * P:k * N + (t + 1) * P],
                                              h[:, t, cols(2 * part + k)], ident[:, :])
                elif kind == "wo":
                    if part == 0:
                        pe.wait_ge(oT_ready, i * PAIRS)
                    if static and i == 1:
                        pe.wait_ge(w_lo, 4)
                    for k in range(DC):
                        mm = three(acc[:, :], half(oT, ALL, k, cols(part)), half(wo, ALL, k, ALL), k == 0, k == DC - 1)
                elif kind == "y":
                    if part == 0:
                        pe.wait_ge(h2_ready, i * NT)
                    if static and i == 1:
                        pe.wait_ge(adj_lo, 1)
                    for k in range(2):
                        for t in range(NT):
                            mm = three(acc[:, k * N:(k + 1) * N], half(h2, ALL, t, cols(2 * part + k)),
                                       half(adjT, ALL, t, ALL), t == 0, t == NT - 1)
                elif kind == "w1":
                    if part == 0:
                        pe.wait_ge(drained["y"], (i - 1) * 2)
                    if static and i == 2:
                        pe.wait_ge(w_lo, 5)
                    for k in range(DC):
                        mm = three(acc[:, :], half(yT, ALL, k, cols(part)), half(w1, ALL, k, ALL), k == 0, k == DC - 1)
                mm.then_inc(filled[kind], 1)

            def step(i, r):
                for c in range(PAIRS):
                    g = i * PAIRS + c
                    if isinstance(i, int):
                        setup(i, c)
                    if pair_exists(g - 1):
                        for e in range(2):
                            if pair_exists(g - 2):
                                pe.wait_ge(pT_ready, (g - 2) * 2 + (e + 1))
                            pe.wait_ge(prob_ready, (g - 1) * 2 + (e + 1))
                            for t in range(NT):
                                for m in range(NT):
                                    mm = pe.transpose(probT[e][:, m * N + t * P:m * N + (t + 1) * P],
                                                      prob[:, e, t, cols(m)], ident[:, :])
                            mm.then_inc(probT_filled, 1)
                    if pair_exists(g):
                        pe.wait_ge(drained["qk"], g + 1)
                        if pair_exists(g - 1):
                            pe.wait_ge(logit_ready, g * 2 * NT)
                        else:
                            pe.wait_ge(adj_lo, 1)
                        for t in range(NT):
                            for n, (qa, ka) in enumerate(((0, 0), (0, 1), (1, 0))):
                                for e in range(2):
                                    rowsl = slice(e * HD, (e + 1) * HD)
                                    mm = pe.matmul(score[e][:, t * N:(t + 1) * N], qT[qa][rowsl, c % 2, cols(t)],
                                                   kT[ka][rowsl, c % 2, :], start=(n == 0), stop=(n == 2))
                        mm.then_inc(score_filled, 1)
                    for f in fills_of(i, c):
                        fill(i, r, f)
                    if pair_exists(g - 1):
                        if pair_exists(g - 2):
                            pe.wait_ge(omain_ready, (g - 1) * 2)
                        if isinstance(i, int) and (i, c) == (1, 0):
                            pe.wait_ge(cbias_ready, 2)
                        co = (c - 1) % PAIRS
                        ring = (r if c else r - 1) % 2
                        if c == 1:
                            pe.wait_ge(drained["v"], i * NT + NT)
                        for e in range(2):
                            pe.wait_ge(pT_ready, (g - 1) * 2 + (e + 1))
                            for t in range(NT):
                                for n in range(2):
                                    mm = pe.matmul(attn[:, e * N:(e + 1) * N],
                                                   v[:, ring, t, 2 * co + e, :, :].rearrange("p a d -> p (a d)"),
                                                   pT[n][:, e, t, :], start=(t == 0 and n == 0),
                                                   stop=(t == NT - 1 and n == 1))
                        mm.then_inc(attn_filled, 1)
                    for f in fills_of(i, c, late=True):
                        fill(i, r, f)

            times(pe, step)


_INS = ["x", "adj", "L0_gnn_Wq", "L0_gnn_bq", "L0_gnn_Wk", "L0_gnn_bk", "L0_gnn_Wv", "L0_gnn_bv",
        "L0_gnn_Wo", "L0_gnn_bo", "L1_gnn_weight", "L1_gnn_bias"]


def kernel(**inputs):
    import numpy as _np
    import concourse.bacc as _bacc
    from concourse import mybir as _mybir
    from concourse.bass_utils import run_bass_kernel_spmd as _run

    nc = _bacc.Bacc("TRN2", target_bir_lowering=False, num_devices=1)
    arrays, args = {}, []
    for name in _INS:
        a = _np.ascontiguousarray(inputs[name])
        arrays[f"in_{name}_dram"] = a
        args.append(nc.dram_tensor(f"in_{name}_dram", a.shape, _mybir.dt.from_np(a.dtype), kind="ExternalInput").ap())
    shape = tuple(inputs["x"].shape)
    args.append(nc.dram_tensor("out_0_dram", shape, _mybir.dt.float32, kind="ExternalOutput").ap())
    adjacency_layers(nc, *args)
    r = _run(nc, [arrays], core_ids=[0])
    return r.results[0]["out_0_dram"]
```

```python
from contextlib import ExitStack

import concourse.bass as bass
from concourse import mybir

F32 = mybir.dt.float32
F32R = mybir.dt.float32r
ALU = mybir.AluOpType
ACT = mybir.ActivationFunctionType

P = 128
EPS = 1e-5
MASK = 1e9
HUGE = 3.0e38


def adjacency_layers(nc, x, adj, Wq, bq, Wk, bk, Wv, bv, Wo, bo, W1, b1, out):
    NB, N, D = x.shape
    H = 8
    HD = D // H
    NT = N // P
    DC = D // P
    PAIRS = H // 2
    RING = 4
    SCALE = 1.0 / HD ** 0.5
    assert HD * 2 == P and PAIRS == DC and N * 2 == D and SCALE == 0.125

    FIRST, END = 2, NB - 2
    assert (END - FIRST) % RING == 0

    FILLS = [
        (0, "qk", 0), (0, "v", 0), (0, "y", 0),
        (1, "qk", 0), (1, "v", 1), (1, "wo", 0),
        (2, "qk", 0), (2, "wo", 1), (2, "y", 1), (2, "ht", 0), (2, "ht", 1),
        (3, "qk", 0), (3, "w1", 0), (3, "w1", 1),
    ]
    LATE = [(0, "y", 0)]
    LAG = {"v": 0, "wo": 1, "ht": -1, "w1": 2, "y": 2}
    BANKS = 3

    def exists(batch):
        return not isinstance(batch, int) or 0 <= batch < NB

    def pair_exists(g):
        return not isinstance(g, int) or 0 <= g < NB * PAIRS

    def fill_count(i, f):
        slot, kind, part = FILLS[f]
        if kind == "qk":
            g = i * PAIRS + (slot + 1)
            return g + 1 if pair_exists(g) else None
        return i * 2 + (part + 1 - 2 * LAG[kind]) if exists(i - LAG[kind]) else None

    def fills_of(i, slot, late=False):
        return [f for f, fill in enumerate(FILLS)
                if fill[0] == slot and (fill in LATE) == late and fill_count(i, f) is not None]

    def bank_of(i, f):
        if isinstance(i, int) and not 1 <= i < NB - 1:
            f = sum(fill_count(i, k) is not None for k in range(f))
        return f % BANKS

    def bank_user_before(i, f):
        bank, k, t = bank_of(i, f), f, i
        while True:
            k -= 1
            if k < 0:
                k, t = len(FILLS) - 1, t - 1
                if isinstance(t, int) and t < -1:
                    return None
            if bank_of(t, k) == bank and fill_count(t, k) is not None:
                kind, part = FILLS[k][1:]
                if kind == "w1" and not isinstance(t, int):
                    return kind, t * 2 + (2 - 2 * LAG[kind])
                return kind, fill_count(t, k)

    def times(eng, step):
        for i in range(-1, FIRST):
            step(i, i % RING)
        with eng.Fori(0, (END - FIRST) // RING) as m:
            for j in range(RING):
                step(m * RING + (FIRST + j), (FIRST + j) % RING)
        for i in range(END, NB + 2):
            step(i, i % RING)

    with ExitStack() as ctx:
        def sb(name, shape, dt=F32):
            return ctx.enter_context(nc.sbuf_tensor(name, shape, dt))

        def sem(name):
            return ctx.enter_context(nc.semaphore(name))

        def split_pair(name, shape):
            return sb(name + "_hi", shape, F32R), sb(name + "_lo", shape, F32R)

        wq, wk, wv, wo, w1 = (split_pair(n, [P, DC, D]) for n in ("wq", "wk", "wv", "wo", "w1"))
        adjT = split_pair("adjT", [P, NT, N])
        mask = sb("mask", [P, NT, N])
        cbias = sb("cbias", [P, D])
        obias = sb("obias", [P, D])
        ident = sb("ident", [P, P])
        stage = sb("stage", [P, 2, DC, D])
        bias_rows = sb("bias_rows", [3 * DC, P])
        bias_cols = sb("bias_cols", [P, 3 * DC])
        bqs = sb("bqs", [P, DC])
        bvb = obias[:, :].rearrange("p (c n) -> p c n", c=DC)
        nhalf, eps = sb("nhalf", [P, NT]), sb("eps", [P, NT])

        xr = sb("xr", [P, RING, NT, D])
        h = sb("h", [P, NT, D])
        hT = split_pair("hT", [P, DC, N])
        qT = sb("qT", [P, 2, 2, N], F32R)
        kT = sb("kT", [P, 2, 2, 2, N], F32R)
        v = sb("v", [P, 2, NT, H, 2, HD], F32R)
        logit = sb("logit", [P, 2, NT, N])
        adjn = logit[:, 0, :, :]
        low = sb("low", [P, 2 * NT])
        prob = sb("prob", [P, 2, NT, N])
        total = sb("total", [P, 2 * NT])
        rtotal = sb("rtotal", [P, 2 * NT])
        pT = split_pair("pT", [P, 2, NT, N])
        oT = split_pair("oT", [P, DC, N])
        omain, orest = sb("omain", [P, N]), sb("orest", [P, N])
        z = stage[:, 0, 0:NT, :]
        h2 = split_pair("h2", [P, NT, D])
        yT = split_pair("yT", [P, DC, N])
        st1 = sb("st1", [P, NT, 6]); mv1 = sb("mv1", [P, NT, 2]); rs1 = sb("rs1", [P, NT]); ve1 = sb("ve1", [P, NT])
        st2 = sb("st2", [P, NT, 6]); mv2 = sb("mv2", [P, NT, 2]); rs2 = sb("rs2", [P, NT]); ve2 = sb("ve2", [P, NT])

        def bank(name):
            return ctx.enter_context(nc.psum_tensor(name, [P, 512], F32))
        dense = [bank(f"dense{b}") for b in range(BANKS)]
        score = [bank(f"score{e}") for e in range(2)]
        probT = [bank(f"probT{e}") for e in range(2)]
        bias_bank = dense[bank_of(1, FILLS.index((0, "y", 0)))]
        attn = bank("attn")

        x_loaded = [sem(f"x_loaded{r}") for r in range(RING)]
        x_stored = [sem(f"x_stored{r}") for r in range(RING)]
        w_loaded = [sem(f"w_loaded{n}") for n in range(9)]
        adj_loaded, bias_loaded = sem("adj_loaded"), sem("bias_loaded")
        ident_ready, powers_ready = sem("ident_ready"), sem("powers_ready")
        bo_loaded, b1_loaded = sem("bo_loaded"), sem("b1_loaded")
        w_hi, w_lo = sem("w_hi"), sem("w_lo")
        adj_turned, adj_hi, adj_lo = sem("adj_turned"), sem("adj_hi"), sem("adj_lo")
        mask_ready, bias_ready = sem("mask_ready"), sem("bias_ready")
        bias_turned, bias_cols_ready = sem("bias_turned"), sem("bias_cols_ready")
        bias_filled, cbias_ready = sem("bias_filled"), sem("cbias_ready")
        KINDS = ("qk", "v", "wo", "ht", "w1", "y")
        filled = {k: sem(f"{k}_filled") for k in KINDS}
        hi_done = {k: sem(f"{k}_hi_done") for k in ("qk", "v", "ht", "y")}
        drained = {k: sem(f"{k}_drained") for k in KINDS}
        k_ready, k_doubled = sem("k_ready"), sem("k_doubled")
        score_filled, logit_ready, exp_done = sem("score_filled"), sem("logit_ready"), sem("exp_done")
        rtotal_ready, prob_ready = sem("rtotal_ready"), sem("prob_ready")
        probT_filled, pT_hi_done, pT_ready = sem("probT_filled"), sem("pT_hi_done"), sem("pT_ready")
        attn_filled, orest_ready, omain_ready = sem("attn_filled"), sem("orest_ready"), sem("omain_ready")
        oT_hi_done, oT_ready = sem("oT_hi_done"), sem("oT_ready")
        stats1, mv1_ready, rs1_ready, h_ready, xc_ready = (sem(n) for n in ("stats1", "mv1_ready", "rs1_ready", "h_ready", "xc_ready"))
        stats2, mv2_ready, rs2_ready, z_ready, xb_ready = (sem(n) for n in ("stats2", "mv2_ready", "rs2_ready", "z_ready", "xb_ready"))
        var1_ready, var2_ready = sem("var1_ready"), sem("var2_ready")
        h2_hi_done, h2_ready = sem("h2_hi_done"), sem("h2_ready")

        staged = [stage[:, 0, :, :], stage[:, 1, :, :],
                  xr[:, 2:4, :, :].rearrange("p a b d -> p (a b) d"), stage[:, 0, :, :], stage[:, 1, :, :]]

        def f32(ap):
            return ap.bitcast(F32)

        WEIGHTS = [(wq, Wq, -SCALE), (wk, Wk, 1.0), (wv, Wv, 1.0), (wo, Wo, 1.0), (w1, W1, 1.0)]
        PIECES = [(0, 0, P), (1, 0, P), (0, P, D), (1, P, D), (2, 0, D),
                  (3, 0, 2 * P), (3, 2 * P, D), (4, 0, 2 * P), (4, 2 * P, D)]

        block = ctx.enter_context(nc.Block())

        @block.sync
        def _(sp):
            def load_x(b, r):
                sp.dma_start(xr[:, r, :, :], x[b].rearrange("(t p) d -> p t d", p=P)).then_inc(x_loaded[r], 16)

            def load_w(piece):
                n, a, b = PIECES[piece]
                sp.dma_start(staged[n][:, :, a:b], WEIGHTS[n][1][:, a:b].rearrange("(c p) n -> p c n", p=P)).then_inc(w_loaded[piece], 16)

            load_x(0, 0)
            for n, b in enumerate((bq, bk, bv)):
                sp.dma_start(bias_rows[n * DC:(n + 1) * DC, :], b.rearrange("(c p) -> c p", p=P)).then_inc(bias_loaded, 16)
            load_w(0)
            load_w(1)
            sp.dma_start(adjn[:, :, :], adj.rearrange("(t p) m -> p t m", p=P)).then_inc(adj_loaded, 16)
            for piece in (2, 3, 4):
                load_w(piece)
            load_x(1, 1)

            sp.wait_ge(w_lo, 3)
            load_w(5)
            load_w(6)
            sp.wait_ge(w_lo, 4)
            load_w(7)
            load_w(8)
            sp.wait_ge(w_lo, 5)
            load_x(2, 2)
            load_x(3, 3)

            def step(i, r):
                if exists(i - 2):
                    sp.wait_ge(drained["w1"], (i - 2) * NT + NT)
                    s = (r - 2) % RING
                    sp.dma_start(out[i - 2].rearrange("(t p) d -> p t d", p=P), xr[:, s, :, :]).then_inc(x_stored[s], 16)
                    if exists(i + 2):
                        sp.wait_ge(x_stored[s], (i - 2) * 4 + (16 - 4 * s))
                        load_x(i + 2, s)

            times(sp, step)
            for s in range(RING):
                sp.wait_ge(x_stored[s], 16 * (NB // RING))

        @block.gpsimd
        def _(pool):
            pool.dma_start(cbias[:, :], bo.partition_broadcast(P)).then_inc(bo_loaded, 16)
            pool.memset(nhalf[:, :], -0.5).then_inc(powers_ready, 1)
            pool.memset(eps[:, :], EPS).then_inc(powers_ready, 1)
            pool.memset(ident[:, :], 0.0).then_inc(ident_ready, 1)
            pool.wait_ge(ident_ready, 1)
            pool.affine_select(out=ident[:, :], in_=ident[:, :], compare_op=ALU.not_equal, fill=1.0,
                               base=0, pattern=[[-1, P]], channel_multiplier=1).then_inc(ident_ready, 1)
            pool.wait_ge(powers_ready, 2)

            def norm_scale(mv, mv_ready, ve, var_ready, rs, rs_ready, n):
                pool.wait_ge(mv_ready, (n + 1) * NT)
                pool.tensor_tensor(ve[:, :], mv[:, :, 1], eps[:, :], ALU.add).then_inc(var_ready, 1)
                pool.wait_ge(var_ready, n + 1)
                pool.tensor_tensor(rs[:, :], ve[:, :], nhalf[:, :], ALU.pow).then_inc(rs_ready, 1)

            def oT_lo(g, c):
                pool.wait_ge(oT_hi_done, g - 1)
                co = (c - 2) % PAIRS
                pool.tensor_tensor(oT[1][:, co, :], omain[:, :], f32(oT[0][:, co, :]), ALU.subtract).then_inc(oT_ready, 1)

            def step(i, r):
                for c in range(PAIRS):
                    g = i * PAIRS + c
                    if pair_exists(g - 2) and c != 2:
                        oT_lo(g, c)
                    if pair_exists(g):
                        for e in range(2):
                            if e == 0:
                                pool.wait_ge(rtotal_ready, g + 1)
                            pool.tensor_tensor(
                                prob[:, e, :, :], prob[:, e, :, :],
                                rtotal[:, e * NT:(e + 1) * NT].unsqueeze(2).to_broadcast((P, NT, N)),
                                ALU.mult).then_inc(prob_ready, 1)
                    if pair_exists(g - 2) and c == 2:
                        oT_lo(g, c)
                    if c == 1 and exists(i + 1):
                        norm_scale(mv1, mv1_ready, ve1, var1_ready, rs1, rs1_ready, i + 1)
                    if c == 3 and exists(i - 1):
                        norm_scale(mv2, mv2_ready, ve2, var2_ready, rs2, rs2_ready, i - 1)
                    if c == 0 and exists(i - 1):
                        pool.wait_ge(h_ready, i * NT)
                        if isinstance(i, int) and i == 1:
                            pool.wait_ge(cbias_ready, 1)
                            pool.dma_start(obias[:, :], b1.partition_broadcast(P)).then_inc(b1_loaded, 16)
                        s = (r - 1) % RING
                        for t in range(NT):
                            pool.tensor_tensor(xr[:, s, t, :], xr[:, s, t, :], cbias[:, :], ALU.add).then_inc(xc_ready, 1)
                    if isinstance(i, int) and (i, c) == (1, 2):
                        pool.wait_ge(b1_loaded, 16)
                    if c == 1 and exists(i - 2):
                        pool.wait_ge(z_ready, (i - 1) * NT)
                        s = (r - 2) % RING
                        for t in range(NT):
                            pool.tensor_tensor(xr[:, s, t, :], xr[:, s, t, :], obias[:, :], ALU.add).then_inc(xb_ready, 1)

            times(pool, step)

        @block.scalar
        def _(act):
            def weight_hi(piece):
                n, a, b = PIECES[piece]
                w, _, scale = WEIGHTS[n]
                act.wait_ge(w_loaded[piece], 16)
                act.activation(w[0][:, :, a:b], staged[n][:, :, a:b], ACT.Copy, scale=scale).then_inc(w_hi, 1)

            def setup(i, c):
                if (i, c) == (-1, 3):
                    weight_hi(0)
                    weight_hi(1)
                    act.wait_ge(adj_turned, 1)
                    act.activation(adjT[0][:, :, :].rearrange("p a b -> p (a b)"), score[0][:, :], ACT.Copy).then_inc(adj_hi, 1)
                    for piece in (2, 3):
                        weight_hi(piece)
                    act.wait_ge(bias_ready, 1)

            def setup_late(i, c):
                if (i, c) == (-1, 3):
                    weight_hi(4)
                if (i, c) == (0, 1):
                    weight_hi(5)
                if (i, c) == (0, 2):
                    weight_hi(6)
                if (i, c) == (0, 3):
                    weight_hi(7)
                if (i, c) == (1, 0):
                    weight_hi(8)

            def hi_of_fill(i, r, f):
                slot, kind, part = FILLS[f]
                if kind not in hi_done:
                    return
                acc = dense[bank_of(i, f)]
                count = fill_count(i, f)
                act.wait_ge(filled[kind], count)
                if kind == "qk":
                    c, ring = (slot + 1) % PAIRS, (slot + 1) % 2
                    for e in range(2):
                        own = slice(e * HD, (e + 1) * HD)
                        act.activation(qT[own, ring, e, :], acc[own, 0:N], ACT.Identity, bias=bqs[own, c:c + 1])
                        a = act.activation(kT[own, ring, e, 0, :], acc[own, N:2 * N], ACT.Identity,
                                           bias=bias_cols[own, DC + c:DC + c + 1])
                        a.then_inc(hi_done[kind], 1)
                    for e in range(2):
                        own, other = slice(e * HD, (e + 1) * HD), slice((1 - e) * HD, (2 - e) * HD)
                        act.wait_ge(k_ready, (count - 1) * 2 + (e + 1))
                        act.activation(kT[other, ring, e, :, :], f32(kT[own, ring, e, :, :]), ACT.Copy).then_inc(k_doubled, 1)
                elif kind == "v":
                    act.activation(v[:, r % 2, part, :, 0, :], acc[:, :].rearrange("p (h d) -> p h d", h=H), ACT.Copy).then_inc(hi_done[kind], 1)
                elif kind == "ht":
                    act.activation(hT[0][:, 2 * part:2 * part + 2, :].rearrange("p a b -> p (a b)"), acc[:, :],
                                   ACT.Relu).then_inc(hi_done[kind], 1)
                elif kind == "y":
                    act.activation(yT[0][:, 2 * part:2 * part + 2, :].rearrange("p a b -> p (a b)"), acc[:, :],
                                   ACT.Copy).then_inc(hi_done[kind], 1)

            def oT_hi(g, c):
                act.wait_ge(omain_ready, (g - 1) * 2)
                act.activation(oT[0][:, (c - 2) % PAIRS, :], omain[:, :], ACT.Copy).then_inc(oT_hi_done, 1)

            def step(i, r):
                for c in range(PAIRS):
                    g = i * PAIRS + c
                    if isinstance(i, int):
                        setup(i, c)
                    if pair_exists(g - 1):
                        for e in range(2):
                            act.wait_ge(probT_filled, (g - 1) * 2 + (e + 1))
                            act.activation(pT[0][:, e, :, :].rearrange("p a b -> p (a b)"), probT[e][:, :],
                                           ACT.Copy).then_inc(pT_hi_done, 1)
                    if pair_exists(g - 2) and c != 2:
                        oT_hi(g, c)
                    if pair_exists(g):
                        for e in range(2):
                            for t in range(NT):
                                k = e * NT + t
                                act.wait_ge(logit_ready, g * 2 * NT + (k + 1))
                                act.activation(prob[:, e, t, :], logit[:, e, t, :], ACT.Exp, bias=low[:, k:k + 1],
                                               scale=-1.0, accum_out=total[:, k:k + 1]).then_inc(exp_done, 1)
                    fills = fills_of(i, c)
                    first = sum(FILLS[f][1] == "qk" for f in fills)
                    for f in fills[:first]:
                        hi_of_fill(i, r, f)
                    if pair_exists(g - 2) and c == 2:
                        if exists(i - 1):
                            act.wait_ge(filled["wo"], i * NT)
                        oT_hi(g, c)
                    for f in fills[first:]:
                        hi_of_fill(i, r, f)
                    if isinstance(i, int):
                        setup_late(i, c)
                    if c == 3 and exists(i - 1):
                        act.wait_ge(z_ready, i * NT)
                        for t in range(NT):
                            act.activation(h2[0][:, t, :], z[:, t, :], ACT.Relu).then_inc(h2_hi_done, 1)
                    if pair_exists(g - 1):
                        act.wait_ge(attn_filled, g)
                        for e in range(2):
                            act.activation(orest[e * HD:(e + 1) * HD, :], attn[HD:P, e * N:(e + 1) * N],
                                           ACT.Copy).then_inc(orest_ready, 1)
                    for f in fills_of(i, c, late=True):
                        hi_of_fill(i, r, f)

            times(act, step)

        @block.vector
        def _(dve):
            def lo(out_lo, acc, hi, inc, op0=ALU.add, scalar=0.0):
                return dve.scalar_tensor_tensor(out=out_lo, in0=acc, scalar=scalar, in1=hi, op0=op0,
                                                op1=ALU.subtract).then_inc(inc, 1)

            def weight_lo(piece):
                n, a, b = PIECES[piece]
                w, _, scale = WEIGHTS[n]
                dve.wait_ge(w_hi, piece + 1)
                dve.scalar_tensor_tensor(out=w[1][:, :, a:b], in0=staged[n][:, :, a:b], scalar=scale,
                                         in1=f32(w[0][:, :, a:b]), op0=ALU.mult, op1=ALU.subtract).then_inc(w_lo, 1)

            def setup(i, c):
                if (i, c) == (-1, 3):
                    weight_lo(0)
                    weight_lo(1)
                    dve.wait_ge(adj_loaded, 16)
                    dve.tensor_scalar(mask[:, :, :], adjn[:, :, :], -1.0, 1.0, ALU.mult, ALU.add).then_inc(mask_ready, 1)
                    dve.wait_ge(mask_ready, 1)
                    dve.tensor_scalar(mask[:, :, :], mask[:, :, :], MASK, None, ALU.mult).then_inc(mask_ready, 1)
                    dve.wait_ge(bias_turned, 1)
                    dve.tensor_copy(bias_cols[:, :], score[1][:, 0:3 * DC]).then_inc(bias_cols_ready, 1)
                    dve.wait_ge(adj_hi, 1)
                    lo(adjT[1][:, :, :].rearrange("p a b -> p (a b)"), score[0][:, :],
                       f32(adjT[0][:, :, :]).rearrange("p a b -> p (a b)"), adj_lo)
                    dve.wait_ge(bias_cols_ready, 1)
                    dve.tensor_scalar(bqs[:, :], bias_cols[:, 0:DC], -SCALE, None, ALU.mult).then_inc(bias_ready, 1)
                    dve.tensor_copy(bvb[:, :, :], bias_cols[:, 2 * DC:3 * DC].unsqueeze(2)
                                    .to_broadcast((P, DC, P))).then_inc(bias_ready, 1)
                    for piece in (2, 3):
                        weight_lo(piece)

            def setup_late(i, c):
                if (i, c) == (-1, 3):
                    weight_lo(4)
                if (i, c) == (0, 1):
                    weight_lo(5)
                if (i, c) == (0, 2):
                    weight_lo(6)
                if (i, c) == (0, 3):
                    weight_lo(7)
                if (i, c) == (1, 0):
                    weight_lo(8)
                    dve.wait_ge(bo_loaded, 16)
                    dve.wait_ge(bias_filled, 1)
                    dve.tensor_tensor(cbias[:, :], bias_bank[:, :], cbias[:, :], ALU.add).then_inc(cbias_ready, 1)

            def statistics(src, st, stats, n):
                for t in range(NT):
                    dve.bn_stats(st[:, t, :], src[:, t, :]).then_inc(stats, 1)
                dve.wait_ge(stats, (n + 1) * NT)

            def mean_variance(st, mv, mv_ready):
                for t in range(NT):
                    dve.bn_aggr(mv[:, t, :], st[:, t, :]).then_inc(mv_ready, 1)

            def normalise(dst, src, mv, rs, done):
                for t in range(NT):
                    dve.tensor_scalar(dst[:, t, :], src[:, t, :], mv[:, t, 0:1], rs[:, t:t + 1],
                                      ALU.subtract, ALU.mult).then_inc(done, 1)

            def drain_fill(i, r, f):
                slot, kind, part = FILLS[f]
                acc = dense[bank_of(i, f)]
                count = fill_count(i, f)
                if kind == "qk":
                    c, ring = (slot + 1) % PAIRS, (slot + 1) % 2
                    for e in range(2):
                        own, other = slice(e * HD, (e + 1) * HD), slice((1 - e) * HD, (2 - e) * HD)
                        dve.wait_ge(hi_done[kind], (count - 1) * 2 + (e + 1))
                        dve.scalar_tensor_tensor(out=kT[own, ring, e, 1, :], in0=acc[own, N:2 * N],
                                                 scalar=bias_cols[own, DC + c:DC + c + 1],
                                                 in1=f32(kT[own, ring, e, 0, :]), op0=ALU.add,
                                                 op1=ALU.subtract).then_inc(k_ready, 1)
                        a = dve.scalar_tensor_tensor(out=qT[other, ring, e, :], in0=acc[own, 0:N],
                                                     scalar=bqs[own, c:c + 1], in1=f32(qT[own, ring, e, :]),
                                                     op0=ALU.add, op1=ALU.subtract)
                    a.then_inc(drained[kind], 1)
                    return
                dve.wait_ge((hi_done if kind in hi_done else filled)[kind], count)
                if kind == "v":
                    lo(v[:, r % 2, part, :, 1, :], acc[:, :].rearrange("p (h d) -> p h d", h=H),
                       f32(v[:, r % 2, part, :, 0, :]), drained[kind])
                elif kind == "ht":
                    lo(hT[1][:, 2 * part:2 * part + 2, :].rearrange("p a b -> p (a b)"), acc[:, :],
                       f32(hT[0][:, 2 * part:2 * part + 2, :]).rearrange("p a b -> p (a b)"), drained[kind], op0=ALU.max)
                elif kind == "y":
                    lo(yT[1][:, 2 * part:2 * part + 2, :].rearrange("p a b -> p (a b)"), acc[:, :],
                       f32(yT[0][:, 2 * part:2 * part + 2, :]).rearrange("p a b -> p (a b)"), drained[kind])
                elif kind == "wo":
                    s = (r - 1) % RING
                    dve.wait_ge(xc_ready, count)
                    dve.tensor_tensor(xr[:, s, part, :], acc[:, :], xr[:, s, part, :], ALU.add).then_inc(drained[kind], 1)
                elif kind == "w1":
                    s = (r - 2) % RING
                    dve.wait_ge(xb_ready, count)
                    dve.tensor_tensor(xr[:, s, part, :], acc[:, :], xr[:, s, part, :], ALU.add).then_inc(drained[kind], 1)

            def pT_lo(g, e):
                dve.wait_ge(pT_hi_done, g * 2 + (e + 1))
                lo(pT[1][:, e, :, :].rearrange("p a b -> p (a b)"), probT[e][:, :],
                   f32(pT[0][:, e, :, :]).rearrange("p a b -> p (a b)"), pT_ready)

            def step(i, r):
                for c in range(PAIRS):
                    g = i * PAIRS + c
                    if isinstance(i, int):
                        setup(i, c)
                    if isinstance(i, int) and (i, c) == (0, 0):
                        dve.wait_ge(mask_ready, 2)
                    if pair_exists(g):
                        dve.wait_ge(score_filled, g + 1)
                    if pair_exists(g - 1):
                        pT_lo(g - 1, 0)
                    if pair_exists(g):
                        for e in range(2):
                            for t in range(NT):
                                k = e * NT + t
                                dve.tensor_tensor_reduce(
                                    out=logit[:, e, t, :], in0=score[e][:, t * N:(t + 1) * N], in1=mask[:, t, :],
                                    scale=1.0, scalar=HUGE, op0=ALU.add, op1=ALU.min,
                                    accum_out=low[:, k:k + 1]).then_inc(logit_ready, 1)
                    if pair_exists(g - 1):
                        pT_lo(g - 1, 1)
                    if c == 0 and exists(i - 2):
                        for t in range(NT):
                            dve.wait_ge(h2_hi_done, (i - 2) * NT + (t + 1))
                            lo(h2[1][:, t, :], z[:, t, :], f32(h2[0][:, t, :]), h2_ready, op0=ALU.max)
                    if c == 1 and exists(i + 1):
                        n, s = i + 1, (r + 1) % RING
                        dve.wait_ge(x_loaded[s], n * 4 + (16 - 4 * s))
                        statistics(xr[:, s, :, :], st1, stats1, n)
                    if c == 2 and exists(i + 1):
                        s = (r + 1) % RING
                        dve.wait_ge(rs1_ready, i + 2)
                        normalise(h, xr[:, s, :, :], mv1, rs1, h_ready)
                    if c == 3 and exists(i - 1):
                        s = (r - 1) % RING
                        dve.wait_ge(drained["wo"], i * NT)
                        statistics(xr[:, s, :, :], st2, stats2, i - 1)
                    if pair_exists(g):
                        dve.wait_ge(exp_done, (g + 1) * 2 * NT)
                        dve.reciprocal(rtotal[:, :], total[:, :]).then_inc(rtotal_ready, 1)
                    if c == 1 and exists(i + 1):
                        mean_variance(st1, mv1, mv1_ready)
                    if c == 3 and exists(i - 1):
                        mean_variance(st2, mv2, mv2_ready)
                    fills = fills_of(i, c)
                    first = sum(FILLS[f][1] == "qk" for f in fills)
                    for f in fills[:first]:
                        drain_fill(i, r, f)
                    if c == 3 and exists(i - 1):
                        s = (r - 1) % RING
                        dve.wait_ge(rs2_ready, i)
                        normalise(z, xr[:, s, :, :], mv2, rs2, z_ready)
                    for f in fills[first:]:
                        drain_fill(i, r, f)
                    if isinstance(i, int):
                        setup_late(i, c)
                    if pair_exists(g - 1):
                        dve.wait_ge(orest_ready, g * 2)
                        if pair_exists(g - 2):
                            dve.wait_ge(oT_ready, g - 1)
                        for e in range(2):
                            own = slice(e * HD, (e + 1) * HD)
                            dve.tensor_tensor(omain[own, :], attn[0:HD, e * N:(e + 1) * N], orest[own, :],
                                              ALU.add).then_inc(omain_ready, 1)
                    for f in fills_of(i, c, late=True):
                        drain_fill(i, r, f)

            times(dve, step)

        @block.tensor
        def _(pe):
            def three(acc, a, b, first, last):
                pe.matmul(acc, a[0], b[0], start=first, stop=False)
                pe.matmul(acc, a[0], b[1], start=False, stop=False)
                return pe.matmul(acc, a[1], b[0], start=False, stop=last)

            def half(pair, *index):
                return pair[0][index], pair[1][index]

            ALL = slice(None)

            def cols(k, width=P):
                return slice(k * width, (k + 1) * width)

            def setup(i, c):
                if (i, c) == (-1, 2):
                    pe.wait_ge(ident_ready, 2)
                if (i, c) == (-1, 3):
                    pe.wait_ge(bias_loaded, 3 * 16)
                    pe.transpose(score[1][:, 0:3 * DC], bias_rows[:, :], ident[0:3 * DC, 0:3 * DC]).then_inc(bias_turned, 1)
                    pe.wait_ge(adj_loaded, 16)
                    for t in range(NT):
                        for m in range(NT):
                            mm = pe.transpose(score[0][:, m * N + t * P:m * N + (t + 1) * P], adjn[:, t, cols(m)], ident[:, :])
                    mm.then_inc(adj_turned, 1)
                if (i, c) == (1, 3):
                    pe.wait_ge(w_lo, 9)

            def setup_late(i, c):
                if (i, c) == (1, 0):
                    pe.wait_ge(bias_ready, 2)
                    pe.wait_ge(w_loaded[5], 16)
                    pe.wait_ge(w_loaded[6], 16)
                    for k in range(DC):
                        mm = pe.matmul(bias_bank[:, :], bvb[:, k, :], staged[3][:, k, :], start=(k == 0), stop=(k == DC - 1))
                    mm.then_inc(bias_filled, 1)

            def fill(i, r, f):
                slot, kind, part = FILLS[f]
                acc = dense[bank_of(i, f)]
                before = bank_user_before(i, f)
                if before:
                    pe.wait_ge(drained[before[0]], before[1])
                static = isinstance(i, int)
                if kind == "qk":
                    if static and i == -1:
                        pe.wait_ge(w_lo, 2)
                    if static and i == 0:
                        pe.wait_ge(w_lo, 4)
                    if slot == 3:
                        pe.wait_ge(drained["ht"], (i + 2) * 2)
                    c = (slot + 1) % PAIRS
                    for w, at in ((wq, 0), (wk, N)):
                        for k in range(DC):
                            mm = three(acc[:, at:at + N], half(w, ALL, k, cols(c)), half(hT, ALL, k, ALL),
                                       k == 0, k == DC - 1)
                elif kind == "v":
                    if static and i == 0:
                        pe.wait_ge(w_lo, 5)
                    for k in range(DC):
                        mm = three(acc[:, :], half(hT, ALL, k, cols(part)), half(wv, ALL, k, ALL), k == 0, k == DC - 1)
                elif kind == "ht":
                    if part == 0:
                        pe.wait_ge(h_ready, (i + 2) * NT)
                    for k in range(2):
                        for t in range(NT):
                            mm = pe.transpose(acc[:, k * N + t * P:k * N + (t + 1) * P],
                                              h[:, t, cols(2 * part + k)], ident[:, :])
                elif kind == "wo":
                    if static and i == 1:
                        pe.wait_ge(cbias_ready, 1)
                    if part == 0:
                        pe.wait_ge(oT_ready, i * PAIRS)
                    if static and i == 1:
                        pe.wait_ge(w_lo, 7)
                    for k in range(DC):
                        mm = three(acc[:, :], half(oT, ALL, k, cols(part)), half(wo, ALL, k, ALL), k == 0, k == DC - 1)
                elif kind == "y":
                    if part == 0:
                        pe.wait_ge(h2_ready, (i - 1) * NT)
                    for k in range(2):
                        for t in range(NT):
                            mm = three(acc[:, k * N:(k + 1) * N], half(h2, ALL, t, cols(2 * part + k)),
                                       half(adjT, ALL, t, ALL), t == 0, t == NT - 1)
                elif kind == "w1":
                    for k in range(DC):
                        if part == 0 and k % 2 == 0:
                            pe.wait_ge(drained["y"], i * 2 + (k // 2 - 3))
                        mm = three(acc[:, :], half(yT, ALL, k, cols(part)), half(w1, ALL, k, ALL), k == 0, k == DC - 1)
                mm.then_inc(filled[kind], 1)

            def step(i, r):
                for c in range(PAIRS):
                    g = i * PAIRS + c
                    if isinstance(i, int):
                        setup(i, c)
                    if pair_exists(g - 1):
                        for e in range(2):
                            if pair_exists(g - 2):
                                pe.wait_ge(pT_ready, (g - 2) * 2 + (e + 1))
                            pe.wait_ge(prob_ready, (g - 1) * 2 + (e + 1))
                            for t in range(NT):
                                for m in range(NT):
                                    mm = pe.transpose(probT[e][:, m * N + t * P:m * N + (t + 1) * P],
                                                      prob[:, e, t, cols(m)], ident[:, :])
                            mm.then_inc(probT_filled, 1)
                    if pair_exists(g):
                        pe.wait_ge(drained["qk"], g + 1)
                        pe.wait_ge(k_doubled, (g + 1) * 2)
                        if pair_exists(g - 1):
                            pe.wait_ge(logit_ready, g * 2 * NT)
                        else:
                            pe.wait_ge(adj_lo, 1)
                        for e in range(2):
                            for t in range(NT):
                                for n in range(2):
                                    mm = pe.matmul(score[e][:, t * N:(t + 1) * N], qT[:, c % 2, e, cols(t)],
                                                   kT[:, c % 2, e, n, :], start=(n == 0), stop=(n == 1))
                        mm.then_inc(score_filled, 1)
                    for f in fills_of(i, c):
                        fill(i, r, f)
                    if isinstance(i, int):
                        setup_late(i, c)
                    if pair_exists(g - 1):
                        if pair_exists(g - 2):
                            pe.wait_ge(omain_ready, (g - 1) * 2)
                        co = (c - 1) % PAIRS
                        ring = (r if c else r - 1) % 2
                        if c == 1:
                            pe.wait_ge(drained["v"], i * NT + NT)
                        for e in range(2):
                            pe.wait_ge(pT_ready, (g - 1) * 2 + (e + 1))
                            for t in range(NT):
                                for n in range(2):
                                    mm = pe.matmul(attn[:, e * N:(e + 1) * N],
                                                   v[:, ring, t, 2 * co + e, :, :].rearrange("p a d -> p (a d)"),
                                                   pT[n][:, e, t, :], start=(t == 0 and n == 0),
                                                   stop=(t == NT - 1 and n == 1))
                        mm.then_inc(attn_filled, 1)
                    for f in fills_of(i, c, late=True):
                        fill(i, r, f)

            times(pe, step)


_INS = ["x", "adj", "L0_gnn_Wq", "L0_gnn_bq", "L0_gnn_Wk", "L0_gnn_bk", "L0_gnn_Wv", "L0_gnn_bv",
        "L0_gnn_Wo", "L0_gnn_bo", "L1_gnn_weight", "L1_gnn_bias"]


def kernel(**inputs):
    import numpy as _np
    import concourse.bacc as _bacc
    from concourse import mybir as _mybir
    from concourse.bass_utils import run_bass_kernel_spmd as _run

    nc = _bacc.Bacc("TRN2", target_bir_lowering=False, num_devices=1)
    arrays, args = {}, []
    for name in _INS:
        a = _np.ascontiguousarray(inputs[name])
        arrays[f"in_{name}_dram"] = a
        args.append(nc.dram_tensor(f"in_{name}_dram", a.shape, _mybir.dt.from_np(a.dtype), kind="ExternalInput").ap())
    shape = tuple(inputs["x"].shape)
    args.append(nc.dram_tensor("out_0_dram", shape, _mybir.dt.float32, kind="ExternalOutput").ap())
    adjacency_layers(nc, *args)
    r = _run(nc, [arrays], core_ids=[0])
    return r.results[0]["out_0_dram"]
```
